# Optimizing a Trainium2 kernel written in Bass

```python
import numpy as np
import jax
import jax.numpy as jnp

def _softmax(x, axis=-1):
    return jax.nn.softmax(x, axis=axis)

def _gelu(x):
    return jax.nn.gelu(x, approximate=True)

def _silu(x):
    return jax.nn.silu(x)

def _sigmoid(x):
    return jax.nn.sigmoid(x)

def _layernorm(x, axis=-1, eps=1e-05):
    m = jnp.mean(x, axis=axis, keepdims=True)
    v = jnp.var(x, axis=axis, keepdims=True)
    return (x - m) / jnp.sqrt(v + eps)

def _scatter_add(tgt, idx, src, axis=0):
    return tgt.at[idx].add(src)

def _segment_sum(src, seg, n):
    return jax.ops.segment_sum(src, seg, n)
kernel_name = 'mk_adj_ffn_d2_adj_r2_eb4aef'

def setup_inputs(seed: int=0):
    np.random.seed(seed)
    _w = jnp.asarray

    def _rec_inputs():
        import jax
        import jax.numpy as jnp
        _gk = jax.random.key(seed)
        x = -0.0005207 + 1.001 * jax.random.normal(jax.random.fold_in(_gk, 1), (8192, 128), jnp.float32)
        _a = jax.random.bernoulli(jax.random.fold_in(_gk, 2), 0.000488281, (8192, 8192))
        _a = jnp.logical_or(_a, jnp.swapaxes(_a, -1, -2))
        _a = jnp.logical_or(_a, jnp.eye(8192, dtype=bool))
        _af = _a.astype(jnp.float32)
        _af = _af * jax.random.uniform(jax.random.fold_in(_gk, 3), (8192, 8192), jnp.float32, 0.05, 1)
        adj = _af
        return (x, adj)
    x, adj = _rec_inputs()

    def _L0_gnn_setup():
        import jax, jax.numpy as jnp
        import numpy as np
        N = 4096
        D_IN = 128
        D_OUT = 128
        key = jax.random.key(seed)
        k1, k2, k3 = jax.random.split(key, 3)
        input = jax.random.normal(k1, (N, D_IN), dtype=jnp.float32)
        adjacencyMatrix = jax.random.uniform(k2, (N, N), dtype=jnp.float32)
        W = jax.random.normal(k3, (D_OUT, D_IN), dtype=jnp.float32) * (1.0 / np.sqrt(D_IN))
        return {'input': input, 'adjacencyMatrix': adjacencyMatrix, 'W': W}
    _L0_gnn_all = _L0_gnn_setup()
    _L0_gnn_in = {k: v for k, v in _L0_gnn_all.items() if k in ('W',)}
    del _L0_gnn_all

    def _L0_ffn_setup():
        import jax, jax.numpy as jnp
        import numpy as np
        B, T, D, H, E = (16, 2048, 128, 256, 8)
        key = jax.random.key(seed)
        ks = jax.random.split(key, 5)
        x = jax.random.normal(ks[0], (B, T, D), dtype=jnp.float32)
        gate_w = jax.random.normal(ks[1], (D, E), dtype=jnp.float32) * 0.02
        gate_b = jnp.zeros((E,), dtype=jnp.float32)
        W1 = jax.random.normal(ks[2], (E, D, H), dtype=jnp.float32) * 0.02
        b1 = jnp.zeros((E, H), dtype=jnp.float32)
        W2 = jax.random.normal(ks[3], (E, H, D), dtype=jnp.float32) * 0.02
        b2 = jnp.zeros((E, D), dtype=jnp.float32)
        return {'x': x, 'gate_w': gate_w, 'gate_b': gate_b, 'W1': W1, 'b1': b1, 'W2': W2, 'b2': b2}
    _L0_ffn_all = _L0_ffn_setup()
    _L0_ffn_in = {k: v for k, v in _L0_ffn_all.items() if k in ('gate_w', 'gate_b', 'W1', 'b1', 'W2', 'b2')}
    del _L0_ffn_all

    def _L1_gnn_setup():
        import jax, jax.numpy as jnp
        import numpy as np
        N = 4096
        IN_DIM = 128
        OUT_DIM = 128
        key = jax.random.key(seed)
        k1, k2, k3 = jax.random.split(key, 3)
        features = jax.random.normal(k1, (N, IN_DIM), dtype=jnp.float32)
        A = jax.random.uniform(k2, (N, N), dtype=jnp.float32)
        A = A / jnp.sum(A, axis=-1, keepdims=True)
        weight = jax.random.normal(k3, (IN_DIM * 2, OUT_DIM), dtype=jnp.float32) * np.sqrt(6.0 / (IN_DIM * 2 + OUT_DIM))
        bias = jnp.zeros((OUT_DIM,), dtype=jnp.float32)
        return {'features': features, 'A': A, 'weight': weight, 'bias': bias}
    _L1_gnn_all = _L1_gnn_setup()
    _L1_gnn_in = {k: v for k, v in _L1_gnn_all.items() if k in ('weight', 'bias')}
    del _L1_gnn_all

    def _L1_ffn_setup():
        import jax, jax.numpy as jnp
        import numpy as np
        B, S, D, E, H, K = (4, 2048, 128, 8, 256, 2)
        key = jax.random.key(seed)
        ks = jax.random.split(key, 6)
        x = jax.random.normal(ks[0], (B, S, D), jnp.float32)
        Wg = jax.random.normal(ks[1], (D, E), jnp.float32) * 0.02
        bg = jnp.zeros((E,), jnp.float32)
        W1 = jax.random.normal(ks[2], (E, D, H), jnp.float32) * 0.02
        b1 = jnp.zeros((E, H), jnp.float32)
        W2 = jax.random.normal(ks[3], (E, H, D), jnp.float32) * 0.02
        b2 = jnp.zeros((E, D), jnp.float32)
        return {'x': x, 'Wg': Wg, 'bg': bg, 'W1': W1, 'b1': b1, 'W2': W2, 'b2': b2}
    _L1_ffn_all = _L1_ffn_setup()
    _L1_ffn_in = {k: v for k, v in _L1_ffn_all.items() if k in ('Wg', 'bg', 'W1', 'b1', 'W2', 'b2')}
    del _L1_ffn_all
    return {'x': x, 'adj': adj, 'L0_gnn_W': _L0_gnn_in['W'], 'L0_ffn_gate_w': _L0_ffn_in['gate_w'], 'L0_ffn_gate_b': _L0_ffn_in['gate_b'], 'L0_ffn_W1': _L0_ffn_in['W1'], 'L0_ffn_b1': _L0_ffn_in['b1'], 'L0_ffn_W2': _L0_ffn_in['W2'], 'L0_ffn_b2': _L0_ffn_in['b2'], 'L1_gnn_weight': _L1_gnn_in['weight'], 'L1_gnn_bias': _L1_gnn_in['bias'], 'L1_ffn_Wg': _L1_ffn_in['Wg'], 'L1_ffn_bg': _L1_ffn_in['bg'], 'L1_ffn_W1': _L1_ffn_in['W1'], 'L1_ffn_b1': _L1_ffn_in['b1'], 'L1_ffn_W2': _L1_ffn_in['W2'], 'L1_ffn_b2': _L1_ffn_in['b2']}

def reference(x, adj, L0_gnn_W, L0_ffn_gate_w, L0_ffn_gate_b, L0_ffn_W1, L0_ffn_b1, L0_ffn_W2, L0_ffn_b2, L1_gnn_weight, L1_gnn_bias, L1_ffn_Wg, L1_ffn_bg, L1_ffn_W1, L1_ffn_b1, L1_ffn_W2, L1_ffn_b2):
    import jax
    import jax.numpy as jnp

    def _L0_gnn_ref(input, adjacencyMatrix, W):
        import jax, jax.numpy as jnp
        import numpy as np
        N = 4096
        D_IN = 128
        D_OUT = 128
        d_inv_sqrt = jnp.sum(adjacencyMatrix, axis=1) ** (-0.5)
        A_norm = adjacencyMatrix * d_inv_sqrt[:, None] * d_inv_sqrt[None, :]
        h = A_norm @ input
        return h @ W.T

    def _L0_ffn_ref(x, gate_w, gate_b, W1, b1, W2, b2):
        import jax, jax.numpy as jnp
        import numpy as np
        B, T, D, H, E = (16, 2048, 128, 256, 8)
        Bb, Tt, Dd = x.shape
        Ee = gate_w.shape[1]
        xf = x.reshape(-1, Dd)
        N = xf.shape[0]
        logits = xf @ gate_w + gate_b
        probs = jax.nn.softmax(logits, axis=-1)
        top2_vals, top2_idx = jax.lax.top_k(probs, 2)
        cw = jnp.zeros((N, Ee), dtype=xf.dtype).at[jnp.arange(N)[:, None], top2_idx].add(top2_vals)

        def step(acc, params):
            w1, bb1, w2, bb2, we = params
            h = jax.nn.gelu(xf @ w1 + bb1, approximate=False)
            y = h @ w2 + bb2
            return (acc + we[:, None] * y, None)
        out, _ = jax.lax.scan(step, jnp.zeros_like(xf), (W1, b1, W2, b2, cw.T))
        return out.reshape(Bb, Tt, Dd)

    def _L1_gnn_ref(features, A, weight, bias):
        import jax, jax.numpy as jnp
        import numpy as np
        N = 4096
        IN_DIM = 128
        OUT_DIM = 128
        agg_feats = jnp.matmul(A, features)
        cat_feats = jnp.concatenate([features, agg_feats], axis=-1)
        out = jnp.einsum('nd,df->nf', cat_feats, weight)
        return jax.nn.relu(out + bias)

    def _L1_ffn_ref(x, Wg, bg, W1, b1, W2, b2):
        import jax, jax.numpy as jnp
        import numpy as np
        B, S, D, E, H, K = (4, 2048, 128, 8, 256, 2)
        Bv, Sv, Dv = x.shape
        gate_scores = x @ Wg + bg
        _, idx = jax.lax.top_k(gate_scores, K)
        mask = jax.nn.one_hot(idx, E, dtype=x.dtype).sum(axis=-2)
        xf = x.reshape(-1, Dv)
        mf = mask.reshape(-1, E)
        h = jax.nn.gelu(jnp.einsum('td,edh->teh', xf, W1) + b1[None], approximate=False)
        y = jnp.einsum('teh,ehd->ted', h, W2) + b2[None]
        out = jnp.einsum('ted,te->td', y, mf)
        return out.reshape(Bv, Sv, Dv)
    x = x + _L0_gnn_ref(_layernorm(x, axis=-1), adj, L0_gnn_W)
    x = x + _L0_ffn_ref(_layernorm(x, axis=-1)[None], L0_ffn_gate_w, L0_ffn_gate_b, L0_ffn_W1, L0_ffn_b1, L0_ffn_W2, L0_ffn_b2)[0]
    x = x + _L1_gnn_ref(_layernorm(x, axis=-1), adj, L1_gnn_weight, L1_gnn_bias)
    x = x + _L1_ffn_ref(_layernorm(x, axis=-1)[None], L1_ffn_Wg, L1_ffn_bg, L1_ffn_W1, L1_ffn_b1, L1_ffn_W2, L1_ffn_b2)[0]
    return x

_drawn_inputs = setup_inputs


def setup_inputs(seed=0):
    import zlib

    import numpy as np

    out = dict(_drawn_inputs(seed))
    spreads = {'L0_ffn_gate_b': (0.0, 0.342),
     'L0_ffn_b1': (0.0, 0.8),
     'L0_ffn_b2': (0.0, 0.1),
     'L1_gnn_bias': (0.0, 0.1),
     'L1_ffn_bg': (0.0, 0.1),
     'L1_ffn_b1': (0.0, 0.778),
     'L1_ffn_b2': (0.0, 0.1)}
    factors = {'L0_ffn_gate_w': 2.695, 'L0_ffn_W1': 5.696, 'L0_ffn_W2': 4.885}
    for name, (base, spread) in spreads.items():
        noise = np.random.default_rng([zlib.crc32(name.encode()), seed]).standard_normal(out[name].shape)
        drawn = base * np.exp(spread * noise) if base else spread * noise
        out[name] = jnp.asarray(drawn.astype(out[name].dtype))
    for name, factor in factors.items():
        out[name] = (out[name] * factor).astype(out[name].dtype)
    return out
```

```python
from contextlib import ExitStack

import numpy as np
import concourse.bass as bass
from concourse import mybir

F32 = mybir.dt.float32
F32R = mybir.dt.float32r
ALU = mybir.AluOpType
ACT = mybir.ActivationFunctionType
AX = mybir.AxisListType

P = 128
N = 8192
D = 128
E = 8
H = 256
TOPK = 2
PW = 1024
NP = N // PW
JB = N // P
TT = PW // P
CH = 512
CT = CH // P
NC = PW // CH
RING = 4
WT = 2 * E * H // PW
UNITS = NC * E
LEAD = 3
LN_EPS = 1e-5
ROW_TILES = NP * TT * 8


def schedule(product, experts, last_of_layer=False, lead=0):
    at = {}

    def put(pos, what):
        at.setdefault(pos, []).append(what)

    if experts:
        put(-1, ("acc",))
        put(2, ("own",))
        put(4, ("graph_out",))
        put(12, ("turn",))
        put(15, ("gate",))
        put(21, ("weights_turn",))
        for u in range(UNITS):
            put(23 + 2 * u, ("unit", u))
        end = 55 if last_of_layer else 57
        put(55, ("drain", UNITS - 2))
        put(end, ("drain", UNITS - 1))
        put(55 if last_of_layer else 59, ("add", NC - 1))
    if last_of_layer:
        for p in range(NP - 1):
            for half in range(NC):
                put(8 * p + 4 * half - 1 - (0 if p + half == 0 else 3), ("next", p, half))
        for half in range(NC):
            put(55, ("next", NP - 1, half))
    tiles = range(JB) if product else ()
    for pos in range(-LEAD - 4, JB + LEAD):
        if product and 0 <= pos < JB:
            yield ("tile", pos)
        for what in at.get(pos - lead, ()) if pos < JB - 1 or not product else ():
            yield what
        if product and pos == JB - 1:
            for late in range(pos - lead, JB):
                yield from at.get(late, ())
            return


class Steps:

    def __init__(self, eng, sem):
        self.eng, self.sem, self.done, self.shift = eng, sem, 0, None

    def loop(self, var, first, per, times):
        self.shift, self.start, self.per, self.times = (var - first) * per, self.done, per, times

    def end_loop(self):
        assert self.done == self.start + self.per, (self.done - self.start, self.per)
        self.done, self.shift = self.start + self.per * self.times, None

    def wait(self, ins):
        ins.then_inc(self.sem, 1)
        self.done += 1
        self.eng.wait_ge(self.sem, self.done if self.shift is None else self.shift + self.done)


def two_layers(nc, x, adj_rows, adj_cols, w_gnn0, w_gnn1_own, w_gnn1_agg, bias_gnn1, w_experts,
               b1, b2, w_gate, b_gate, ident_in, select_in, below_in, out):
    ctx = ExitStack()
    with ctx:
        def sb(name, shape, dt=F32):
            return ctx.enter_context(nc.sbuf_tensor(name, shape, dt))

        def sem(name):
            return ctx.enter_context(nc.semaphore(name))

        xs = sb("xs", [P, JB, D])
        y_hi = sb("y_hi", [P, JB, D], F32R)
        y_lo = sb("y_lo", [P, JB, D], F32R)
        raw = sb("raw", [P, RING, PW])
        a_hi = sb("a_hi", [P, RING, PW], F32R)
        a_lo = sb("a_lo", [P, RING, PW], F32R)
        w_hi = sb("w_hi", [P, WT, PW], F32R)
        w_lo = sb("w_lo", [P, WT, PW], F32R)
        xn = sb("xn", [P, TT, D])
        xt_hi = sb("xt_hi", [P, NC, CH], F32R)
        xt_lo = sb("xt_lo", [P, NC, CH], F32R)
        act = sb("act", [P, 2, CH])
        g_hi = sb("g_hi", [P, 4, CH], F32R)
        g_lo = sb("g_lo", [P, 4, CH], F32R)
        turn = sb("turn", [P, CT, D])
        cw_t = sb("cw_t", [2 * E, NC, CH], F32R)
        wg0 = sb("wg0", [P, D])
        wg1_agg = sb("wg1_agg", [P, D])
        wg1_own_hi = sb("wg1_own_hi", [P, D], F32R)
        wg1_own_lo = sb("wg1_own_lo", [P, D], F32R)
        bias1 = sb("bias1", [P, D])
        ident = sb("ident", [P, P])
        gate = sb("gate", [P, 2 * E])
        gate_hi = sb("gate_hi", [P, 2 * E], F32R)
        gate_lo = sb("gate_lo", [P, 2 * E], F32R)
        gate_b = sb("gate_b", [P, 2 * E])
        eb1 = sb("eb1", [P, 2, 2 * E])
        eb2_hi = sb("eb2_hi", [2 * E, 2, D], F32R)
        eb2_lo = sb("eb2_lo", [2 * E, 2, D], F32R)
        select = sb("select", [2 * E, E])
        select_r = sb("select_r", [2 * E, E], F32R)
        below = sb("below", [P, E * E])
        sums = sb("sums", [P, TT, 8])
        d_is = sb("d_is", [P, JB])
        deg = sb("deg", [P, TT])
        stats = sb("stats", [P, TT, 6])
        mv = sb("mv", [P, TT, 2])
        rstd = sb("rstd", [P, TT])
        rscale = sb("rscale", [P, TT])
        pad = sb("pad", [P, 1])
        minus_half = sb("minus_half", [P, TT])
        lg = sb("lg", [P, TT, E])
        pr = sb("pr", [P, TT, E])
        top = sb("top", [P, TT])
        inv = sb("inv", [P, TT])
        rank = sb("rank", [P, TT, E])
        cw = sb("cw", [P, TT, E])
        cw_pair = sb("cw_pair", [P, TT, 2 * E], F32R)
        wg1_own = act[:, 0, 0:D]
        eb2 = act[0:2 * E, 1, 0:2 * D].rearrange("p (l d) -> p l d", l=2)
        acc_s = act[:, :, :]
        cmp_gt = act[:, 0, :].rearrange("p (t a b) -> p t a b", t=TT, a=E)
        cmp_eq = act[:, 1, :].rearrange("p (t a b) -> p t a b", t=TT, a=E)

        acc = ctx.enter_context(nc.psum_tensor("acc", [P, NC, CH], F32))
        hid = ctx.enter_context(nc.psum_tensor("hid", [P, 2, CH], F32))
        cwb = ctx.enter_context(nc.psum_tensor("cwb", [P, CH], F32))
        yps = ctx.enter_context(nc.psum_tensor("yps", [P, CH], F32))
        mix = ctx.enter_context(nc.psum_tensor("mix", [P, NC, CH], F32))

        consts_in = sem("consts_in")
        x_in = sem("x_in")
        landed = [sem(f"landed{i}") for i in range(RING)]
        consts_hi = sem("consts_hi")
        consts_lo = sem("consts_lo")
        row_sum_act = sem("row_sum_act")
        row_sum_dve = sem("row_sum_dve")
        w_hi_made = sem("w_hi_made")
        w_lo_made = sem("w_lo_made")
        a_hi_made = sem("a_hi_made")
        a_lo_made = sem("a_lo_made")
        a_used = sem("a_used")
        y_made = sem("y_made")
        y_hi_made = sem("y_hi_made")
        y_lo_made = sem("y_lo_made")
        acc_saved = sem("acc_saved")
        xn_made = sem("xn_made")
        xt_psum = sem("xt_psum")
        xt_hi_made = sem("xt_hi_made")
        xt_lo_made = sem("xt_lo_made")
        graph_psum = sem("graph_psum")
        graph_added = sem("graph_added")
        gate_psum = sem("gate_psum")
        gate_read = sem("gate_read")
        logits_made = sem("logits_made")
        exp_made = sem("exp_made")
        cw_made = sem("cw_made")
        cwt_psum = sem("cwt_psum")
        cwt_made = sem("cwt_made")
        cwb_psum = sem("cwb_psum")
        hid_psum = sem("hid_psum")
        gelu_made = sem("gelu_made")
        scaled = sem("scaled")
        g_hi_made = sem("g_hi_made")
        g_lo_made = sem("g_lo_made")
        y_done = sem("y_done")
        y_saved = sem("y_saved")
        out_psum = sem("out_psum")
        out_added = sem("out_added")
        dve_step = sem("dve_step")
        half_set = sem("half_set")
        deg_made = sem("deg_made")
        deg_rooted = sem("deg_rooted")
        next_var = sem("next_var")
        next_rstd = sem("next_rstd")
        token_var = sem("token_var")
        token_rstd = sem("token_rstd")
        stored = sem("stored")

        consts = [(wg0, w_gnn0), (wg1_agg, w_gnn1_agg), (wg1_own, w_gnn1_own), (bias1, bias_gnn1),
                  (ident, ident_in), (gate, w_gate), (gate_b, b_gate), (eb1, b1), (eb2, b2),
                  (select, select_in), (below, below_in)]
        splits = [(wg1_own, wg1_own_hi, wg1_own_lo), (gate, gate_hi, gate_lo), (eb2, eb2_hi, eb2_lo)]

        def turns(G, layer, again):
            return G * NC if layer == 0 else NC * NP + (G - NP) * 2 * NC + again * NC

        def tile_use(G, jb):
            return ROW_TILES // RING + WT // RING + (G * JB + jb) // RING if isinstance(G, int) \
                else G * (JB // RING) + (ROW_TILES + WT + jb) // RING

        def panel(t, G, layer, n=TT, first=0):
            if isinstance(G, int):
                a = (G - layer * NP) * TT + first
                return t[:, a:a + n]
            return t[:, bass.ds((G - layer * NP) * TT + first, n)]

        block = ctx.enter_context(nc.Block())

        @block.sync
        def _(sp):
            sp.dma_start(xs[:], x).then_inc(x_in, 16)
            for t, src in consts:
                sp.dma_start(t[:], src).then_inc(consts_in, 16)

            def row_tiles(r, first):
                for c in range(8):
                    if not (first and c < RING):
                        sp.wait_ge(row_sum_dve if c % 2 else row_sum_act, r * 4 + (c - RING) // 2 + 1)
                    src = adj_rows[r, c] if isinstance(r, int) else \
                        adj_rows[bass.ds(r, 1), c].rearrange("o p n -> (o p) n")
                    sp.dma_start(raw[:, c % RING], src).then_inc(landed[c % RING], 16)

            row_tiles(0, True)
            with sp.Fori(1, JB) as r:
                row_tiles(r, False)

            def weight_tiles(layer):
                for i in range(WT):
                    if layer == 0:
                        sp.wait_ge(row_sum_dve if i % 2 else row_sum_act, (ROW_TILES - RING + i) // 2 + 1)
                    else:
                        sp.wait_ge(a_lo_made, (NP + 1) * JB - RING + i + 1)
                    sp.dma_start(raw[:, i], w_experts[layer, i]).then_inc(landed[i], 16)

            def col_tiles(G, layer, skip=0):
                for jb in range(JB):
                    if jb >= skip:
                        sp.wait_ge(a_lo_made, G * JB + jb - RING + 1)
                    src = adj_cols[G - layer * NP, jb] if isinstance(G, int) else \
                        adj_cols[bass.ds(G - layer * NP, 1), jb].rearrange("o p n -> (o p) n")
                    sp.dma_start(raw[:, jb % RING], src).then_inc(landed[jb % RING], 16)

            weight_tiles(0)
            sp.wait_ge(w_lo_made, WT)
            col_tiles(0, 0, skip=RING)
            with sp.Fori(1, NP) as G:
                col_tiles(G, 0)
            col_tiles(NP, 1)
            weight_tiles(1)
            sp.wait_ge(w_lo_made, 2 * WT)
            with sp.Fori(NP + 1, 2 * NP) as G:
                col_tiles(G, 1)
            for p in range(NP):
                for c in range(NC):
                    sp.wait_ge(out_added, (NP + p) * NC + c + 1)
                    a = p * TT + c * CT
                    sp.dma_start(out[:, a:a + CT], xs[:, a:a + CT]).then_inc(stored, 16)
            sp.wait_ge(stored, 16 * NP * NC)

        @block.tensor
        def _(pe):
            def three(o, l_hi, l_lo, r_hi, r_lo, start, stop):
                pe.matmul(o, l_hi, r_hi, start=start, stop=False)
                pe.matmul(o, l_hi, r_lo, start=False, stop=False)
                return pe.matmul(o, l_lo, r_hi, start=False, stop=stop)

            def tile(G, layer, jb, first_panel):
                if jb == 0 and not (isinstance(G, int) and G == 0):
                    pe.wait_ge(acc_saved, G)
                if first_panel and jb % CT == 0:
                    pe.wait_ge(y_lo_made, layer * NP * NC + jb // CT + 1)
                pe.wait_ge(a_lo_made, G * JB + jb + 1)
                s = jb % RING
                for hi_or_lo, left in ((a_hi, y_hi), (a_lo, y_hi), (a_hi, y_lo)):
                    for c in range(NC):
                        mm = pe.matmul(acc[:, c], left[:, jb], hi_or_lo[:, s, c * CH:(c + 1) * CH],
                                       start=(jb == 0 and hi_or_lo is a_hi and left is y_hi),
                                       stop=(jb == JB - 1 and left is y_lo))
                mm.then_inc(a_used, 1)

            def turn_chunks(G, layer, again):
                pe.wait_ge(xn_made, turns(G, layer, again) // NC + 1 if isinstance(G, int) else
                           (G + 1 if layer == 0 else (G - NP) * 2 + (NP + again + 1)))
                for c in range(NC):
                    for t in range(CT):
                        mm = pe.transpose(mix[:, c, t * P:(t + 1) * P], xn[:, c * CT + t], ident[:])
                    mm.then_inc(xt_psum, 1)

            def graph_out(G, layer):
                pe.wait_ge(acc_saved, G + 1)
                if layer == 1:
                    pe.wait_ge(xt_lo_made, turns(G, layer, 0) + NC)
                for c in range(NC):
                    for t in range(CT):
                        o = mix[:, c, t * P:(t + 1) * P]
                        col = slice(t * P, (t + 1) * P)
                        if layer == 1:
                            pe.matmul(o, xt_hi[:, c, col], wg1_own_hi[:], start=True, stop=False)
                            pe.matmul(o, xt_hi[:, c, col], wg1_own_lo[:], start=False, stop=False)
                            pe.matmul(o, xt_lo[:, c, col], wg1_own_hi[:], start=False, stop=False)
                        mm = pe.matmul(o, acc_s[:, c, col], (wg1_agg if layer else wg0)[:],
                                       start=(layer == 0), stop=True)
                    mm.then_inc(graph_psum, 1)

            def gates(G, layer):
                pe.wait_ge(xt_lo_made, turns(G, layer, layer) + NC)
                ge = slice(layer * E, (layer + 1) * E)
                for c in range(NC):
                    for t in range(CT):
                        col = slice(t * P, (t + 1) * P)
                        mm = three(mix[:, c, t * E:(t + 1) * E], xt_hi[:, c, col], xt_lo[:, c, col],
                                   gate_hi[:, ge], gate_lo[:, ge], True, True)
                mm.then_inc(gate_psum, 1)

            def weights_turn(G):
                pe.wait_ge(cw_made, G + 1)
                for c in range(NC):
                    for t in range(CT):
                        mm = pe.transpose(mix[0:2 * E, c, t * P:(t + 1) * P],
                                          cw_pair[:, c * CT + t].bitcast(F32), ident[:])
                    mm.then_inc(cwt_psum, 1)

            def second(G, layer, u):
                c, e = divmod(u, E)
                pe.wait_ge(g_lo_made, (G * UNITS + u) * 2 + 2)
                if e == 0:
                    if c > 0:
                        pe.wait_ge(y_saved, G * NC + c)
                    pe.matmul(yps[:], eb2_hi[:, layer], cw_t[:, c], start=True, stop=False)
                    pe.matmul(yps[:], eb2_lo[:, layer], cw_t[:, c], start=False, stop=False)
                for half in range(2):
                    col = (e * 2 + half) * D
                    l_hi = w_hi[:, WT // 2 + col // PW, col % PW:col % PW + D]
                    l_lo = w_lo[:, WT // 2 + col // PW, col % PW:col % PW + D]
                    s = (2 * u + half) % 4
                    mm = three(yps[:], l_hi, l_lo, g_hi[:, s], g_lo[:, s], False,
                               e == E - 1 and half == 1)
                mm.then_inc(y_done, 1)

            def add(G, c):
                pe.wait_ge(y_saved, G * NC + c + 1)
                for t in range(CT):
                    mm = pe.transpose(mix[:, c, t * P:(t + 1) * P], turn[:, t], ident[:])
                mm.then_inc(out_psum, 1)

            def unit(G, layer, u):
                c, e = divmod(u, E)
                if u == 0:
                    pe.wait_ge(cwt_made, (G + 1) * NC)
                if u > 0:
                    pe.wait_ge(scaled, (G * UNITS + u) * 2)
                pe.matmul(cwb[:], select_r[:, e:e + 1].broadcast_to([2 * E, P]), cw_t[:, c],
                          start=True, stop=True).then_inc(cwb_psum, 1)
                for half in range(2):
                    if u > 0:
                        pe.wait_ge(gelu_made, (G * UNITS + u - 1) * 2 + half + 1)
                    col = e * H + half * P
                    three(hid[:, half], w_hi[:, col // PW, col % PW:col % PW + P],
                          w_lo[:, col // PW, col % PW:col % PW + P], xt_hi[:, c], xt_lo[:, c],
                          True, True).then_inc(hid_psum, 1)
                if u == 0 and layer == 1:
                    pass
                if u >= 2:
                    second(G, layer, u - 2)
                if u == E + 2:
                    add(G, 0)

            def run(G, product, experts, layer, e_layer, first_panel=False, last=False):
                for what, *n in schedule(product, experts, last):
                    if what == "tile":
                        tile(G, layer, n[0], first_panel)
                    elif what == "own" and e_layer == 1:
                        turn_chunks(G - 1, 1, 0)
                    elif what == "graph_out":
                        graph_out(G - 1, e_layer)
                    elif what == "turn":
                        turn_chunks(G - 1, e_layer, e_layer)
                    elif what == "gate":
                        gates(G - 1, e_layer)
                    elif what == "weights_turn":
                        weights_turn(G - 1)
                    elif what == "unit":
                        unit(G - 1, e_layer, n[0])
                    elif what == "drain":
                        second(G - 1, e_layer, n[0])
                    elif what == "add":
                        add(G - 1, n[0])

            pe.wait_ge(consts_lo, 1)
            run(0, True, False, 0, 0, first_panel=True)
            with pe.Fori(1, NP) as G:
                run(G, True, True, 0, 0)
            run(NP, True, True, 1, 0, first_panel=True, last=True)
            pe.wait_ge(w_lo_made, 2 * WT)
            with pe.Fori(NP + 1, 2 * NP) as G:
                run(G, True, True, 1, 1)
            run(2 * NP, False, True, 1, 1)

        @block.scalar
        def _(sc):
            def copy(o, i):
                return nc.scalar.activation(o, i, ACT.Copy)

            sc.wait_ge(consts_in, 16 * len(consts))
            copy(select_r[:], select[:])
            for full, hi, _ in splits:
                ins = copy(hi[:], full[:])
            ins.then_inc(consts_hi, 1)

            def next_y(count, p, layer, half):
                sc.wait_ge(y_made, count + 1)
                copy(panel(y_hi, p, layer, CT, half * CT), turn[:]).then_inc(y_hi_made, 1)

            def rows_of(p, first):
                for t in range(TT):
                    for c in range(0, 8, 2):
                        if t == 0 and c == 0 and not first:
                            sc.wait_ge(deg_made, p)
                        s = c % RING
                        sc.wait_ge(landed[s], (p * (TT * 8 // RING) + (t * 8 + c) // RING + 1) * 16)
                        nc.scalar.activation(raw[:, s], raw[:, s], ACT.Copy,
                                             accum_out=sums[:, t, c:c + 1]).then_inc(row_sum_act, 1)
                for half in range(NC):
                    next_y(p * NC + half, p, 0, half)

            rows_of(0, True)
            with sc.Fori(1, NP) as p:
                rows_of(p, False)

            def weights(layer):
                for i in range(WT):
                    n = ROW_TILES // RING if layer == 0 else tile_use(NP + 1, 0)
                    sc.wait_ge(landed[i], (n + 1) * 16)
                    copy(w_hi[:, i], raw[:, i]).then_inc(w_hi_made, 1)

            def tile(G, jb, shift):
                s = jb % RING
                sc.wait_ge(landed[s], (tile_use(G, jb) + 1 + shift) * 16)
                if not (isinstance(G, int) and G == 0 and jb < RING):
                    sc.wait_ge(a_used, G * JB + jb - RING + 1)
                copy(a_hi[:, s], raw[:, s]).then_inc(a_hi_made, 1)

            def turned(G, layer, again):
                for c in range(NC):
                    sc.wait_ge(xt_psum, turns(G, layer, again) + c + 1)
                    copy(xt_hi[:, c], mix[:, c]).then_inc(xt_hi_made, 1)

            def unit(G, layer, u):
                for half in range(2):
                    v = (G * UNITS + u) * 2 + half
                    sc.wait_ge(hid_psum, v + 1)
                    if u > 0:
                        sc.wait_ge(g_lo_made, v - 1)
                    nc.scalar.activation(act[:, half], hid[:, half], ACT.Gelu,
                                         bias=eb1[:, layer, (u % E) * 2 + half:(u % E) * 2 + half + 1]
                                         ).then_inc(gelu_made, 1)
                for half in range(2):
                    v = (G * UNITS + u) * 2 + half
                    sc.wait_ge(scaled, v + 1)
                    if u >= 2:
                        sc.wait_ge(y_done, G * UNITS + u - 1)
                    copy(g_hi[:, (2 * u + half) % 4], act[:, half]).then_inc(g_hi_made, 1)

            def save_y(G, c):
                sc.wait_ge(y_done, G * UNITS + (c + 1) * E)
                if c > 0:
                    sc.wait_ge(out_psum, G * NC + c)
                copy(turn[:].rearrange("p t d -> p (t d)"), yps[:]).then_inc(y_saved, 1)

            def run(G, product, experts, layer, e_layer, last=False, shift=0):
                for what, *n in schedule(product, experts, last, LEAD if product else 0):
                    if what == "tile":
                        tile(G, n[0], shift)
                    elif what == "acc":
                        sc.wait_ge(a_used, G * JB)
                        copy(acc_s, acc[:]).then_inc(acc_saved, 1)
                    elif what == "own" and e_layer == 1:
                        turned(G - 1, 1, 0)
                    elif what == "turn":
                        turned(G - 1, e_layer, e_layer)
                    elif what == "gate" and e_layer == 0:
                        sc.wait_ge(logits_made, G)
                        nc.scalar.activation(pr[:], lg[:], ACT.Exp).then_inc(exp_made, 1)
                    elif what == "weights_turn":
                        for c in range(NC):
                            sc.wait_ge(cwt_psum, (G - 1) * NC + c + 1)
                            copy(cw_t[:, c], mix[0:2 * E, c]).then_inc(cwt_made, 1)
                    elif what == "unit":
                        unit(G - 1, e_layer, n[0])
                        if n[0] == E + 1:
                            save_y(G - 1, 0)
                    elif what == "drain" and n[0] == UNITS - 1:
                        save_y(G - 1, 1)
                    elif what == "next":
                        next_y(NP * NC + n[0] * NC + n[1], n[0] + NP, 1, n[1])

            weights(0)
            run(0, True, False, 0, 0)
            with sc.Fori(1, NP) as G:
                run(G, True, True, 0, 0)
            run(NP, True, True, 1, 0, last=True)
            weights(1)
            with sc.Fori(NP + 1, 2 * NP) as G:
                run(G, True, True, 1, 1, shift=WT // RING)
            run(2 * NP, False, True, 1, 1)

        @block.gpsimd
        def _(pool):
            def root(t, n, made, done, count):
                pool.wait_ge(made, count + 1)
                nc.gpsimd.tensor_tensor(t[:, 0:n], t[:, 0:n], minus_half[:, 0:n], ALU.pow).then_inc(done, 1)

            def rows_of(p):
                root(deg, TT, deg_made, deg_rooted, p)
                for half in range(NC):
                    root(rstd, CT, next_var, next_rstd, p * NC + half)

            def unit(G, u):
                for half in range(2):
                    v = (G * UNITS + u) * 2 + half
                    pool.wait_ge(g_hi_made, v + 1)
                    s = (2 * u + half) % 4
                    nc.gpsimd.tensor_tensor(g_lo[:, s], act[:, half], g_hi[:, s].bitcast(F32),
                                            ALU.subtract).then_inc(g_lo_made, 1)

            def run(G, last=False):
                for what, *n in schedule(True, True, last, LEAD):
                    if what == "graph_out":
                        root(rstd, TT, token_var, token_rstd, G - 1)
                    elif what == "unit":
                        unit(G - 1, n[0])
                    elif what == "next":
                        root(rstd, CT, next_var, next_rstd, NP * NC + n[0] * NC + n[1])

            nc.gpsimd.memset(minus_half[:], -0.5).then_inc(half_set, 1)
            pool.wait_ge(half_set, 1)
            with pool.Fori(0, NP) as p:
                rows_of(p)
            with pool.Fori(1, NP) as G:
                run(G)
            run(NP, last=True)
            with pool.Fori(NP + 1, 2 * NP + 1) as G:
                run(G)

        @block.vector
        def _(ve):
            v = nc.vector
            steps = Steps(ve, dve_step)

            ve.wait_ge(consts_hi, 1)
            for full, hi, lo in splits:
                ins = v.tensor_tensor(lo[:], full[:], hi[:].bitcast(F32), ALU.subtract)
            ins.then_inc(consts_lo, 1)
            ve.wait_ge(x_in, 16)

            def moments(p, layer, first, n, var_sem, rstd_sem, count):
                v.memset(pad[:], 0.0)
                for t in range(n):
                    ins = v.bn_stats(stats[:, t], panel(xs, p, layer, 1, first + t).rearrange("p o d -> p (o d)"))
                steps.wait(ins)
                v.memset(pad[:], 0.0)
                for t in range(n):
                    ins = v.bn_aggr(mv[:, t], stats[:, t])
                steps.wait(ins)
                v.tensor_scalar(rstd[:, 0:n], mv[:, 0:n, 1], LN_EPS, None, ALU.add).then_inc(var_sem, 1)
                ve.wait_ge(rstd_sem, count + 1)

            def next_y(count, p, layer, half, scale):
                moments(p, layer, half * CT, CT, next_var, next_rstd, count)
                r = rstd
                if scale:
                    steps.wait(v.tensor_tensor(rscale[:, 0:CT], rstd[:, 0:CT],
                                               (d_is[:, half * CT + p * TT:half * CT + p * TT + CT] if isinstance(p, int)
                                                else d_is[:, bass.ds(p * TT + half * CT, CT)]), ALU.mult))
                    r = rscale
                for t in range(CT):
                    ins = v.tensor_scalar(turn[:, t], panel(xs, p, layer, 1, half * CT + t).rearrange("p o d -> p (o d)"),
                                          mv[:, t, 0:1], r[:, t:t + 1], ALU.subtract, ALU.mult)
                ins.then_inc(y_made, 1)
                ve.wait_ge(y_hi_made, count + 1)
                v.tensor_tensor(panel(y_lo, p, layer, CT, half * CT), turn[:],
                                panel(y_hi, p, layer, CT, half * CT).bitcast(F32),
                                ALU.subtract).then_inc(y_lo_made, 1)
                ve.wait_ge(y_lo_made, count + 1)

            def rows_of(p):
                for t in range(TT):
                    for c in range(1, 8, 2):
                        s = c % RING
                        ve.wait_ge(landed[s], (p * (TT * 8 // RING) + (t * 8 + c) // RING + 1) * 16)
                        v.tensor_reduce(sums[:, t, c:c + 1], raw[:, s], AX.X, ALU.add).then_inc(row_sum_dve, 1)
                ve.wait_ge(row_sum_act, (p + 1) * TT * 4)
                ve.wait_ge(row_sum_dve, (p + 1) * TT * 4)
                v.tensor_reduce(deg[:], sums[:], AX.X, ALU.add).then_inc(deg_made, 1)
                ve.wait_ge(deg_rooted, p + 1)
                scale = d_is[:, p * TT:(p + 1) * TT] if isinstance(p, int) else d_is[:, bass.ds(p * TT, TT)]
                steps.wait(v.tensor_copy(scale, deg[:]))
                for half in range(NC):
                    next_y(p * NC + half, p, 0, half, True)

            rows_of(0)
            per = steps.done
            with ve.Fori(1, NP) as p:
                steps.loop(p, 1, per, NP - 1)
                rows_of(p)
                steps.end_loop()

            def weights(layer):
                for i in range(WT):
                    ve.wait_ge(w_hi_made, layer * WT + i + 1)
                    v.tensor_tensor(w_lo[:, i], raw[:, i], w_hi[:, i].bitcast(F32),
                                    ALU.subtract).then_inc(w_lo_made, 1)

            def tile(G, jb):
                s = jb % RING
                ve.wait_ge(a_hi_made, G * JB + jb + 1)
                v.tensor_tensor(a_lo[:, s], raw[:, s], a_hi[:, s].bitcast(F32),
                                ALU.subtract).then_inc(a_lo_made, 1)

            def turned(G, layer, again):
                for c in range(NC):
                    ve.wait_ge(xt_hi_made, turns(G, layer, again) + c + 1)
                    v.tensor_tensor(xt_lo[:, c], mix[:, c], xt_hi[:, c].bitcast(F32),
                                    ALU.subtract).then_inc(xt_lo_made, 1)

            def graph_out(G, layer):
                for c in range(NC):
                    ve.wait_ge(graph_psum, G * NC + c + 1)
                    if layer == 0:
                        for t in range(CT):
                            xt = panel(xs, G, 0, 1, c * CT + t).rearrange("p o d -> p (o d)")
                            col = c * CT + t
                            ds = d_is[:, bass.ds(G * TT + col, 1)] if not isinstance(G, int) else \
                                d_is[:, G * TT + col:G * TT + col + 1]
                            ins = v.scalar_tensor_tensor(xt, mix[:, c, t * P:(t + 1) * P], ds, xt,
                                                         ALU.mult, ALU.add)
                    else:
                        xt = panel(xs, G, 1, CT, c * CT).rearrange("p t d -> p (t d)")
                        m = mix[:, c]
                        for t in range(CT):
                            ins = v.tensor_tensor(mix[:, c, t * P:(t + 1) * P], mix[:, c, t * P:(t + 1) * P],
                                                  bias1[:], ALU.add)
                        steps.wait(ins)
                        ins = v.scalar_tensor_tensor(xt, m, 0.0, xt, ALU.max, ALU.add)
                    steps.wait(ins)
                moments(G, layer, 0, TT, token_var, token_rstd, G)
                for t in range(TT):
                    ins = v.tensor_scalar(xn[:, t], panel(xs, G, layer, 1, t).rearrange("p o d -> p (o d)"),
                                          mv[:, t, 0:1], rstd[:, t:t + 1], ALU.subtract, ALU.mult)
                ins.then_inc(xn_made, 1)

            def gates(G, layer):
                ve.wait_ge(gate_psum, G + 1)
                ge = slice(layer * E, (layer + 1) * E)
                bg = gate_b[:, ge].unsqueeze(1).broadcast_to([P, CT, E])
                for c in range(NC):
                    ins = v.tensor_tensor(lg[:, c * CT:(c + 1) * CT],
                                          mix[:, c, 0:CT * E].rearrange("p (t e) -> p t e", e=E), bg, ALU.add)
                steps.wait(ins)
                score = lg
                if layer == 0:
                    steps.wait(v.tensor_reduce(top[:], lg[:], AX.X, ALU.max))
                    v.tensor_tensor(lg[:], lg[:], top[:].unsqueeze(2).broadcast_to([P, TT, E]),
                                    ALU.subtract).then_inc(logits_made, 1)
                    ve.wait_ge(exp_made, G + 1)
                    steps.wait(v.tensor_reduce(top[:], pr[:], AX.X, ALU.add))
                    steps.wait(v.reciprocal(inv[:], top[:]))
                    steps.wait(v.tensor_tensor(pr[:], pr[:], inv[:].unsqueeze(2).broadcast_to([P, TT, E]),
                                               ALU.mult))
                    score = pr
                other = score[:].unsqueeze(2).broadcast_to([P, TT, E, E])
                own = score[:].unsqueeze(3).broadcast_to([P, TT, E, E])
                v.tensor_tensor(cmp_gt, other, own, ALU.is_gt)
                steps.wait(v.tensor_tensor(cmp_eq, other, own, ALU.is_equal))
                eq = act[:, 1, :].rearrange("p (t n) -> p t n", t=TT)
                steps.wait(v.tensor_tensor(eq, eq, below[:].unsqueeze(1).broadcast_to([P, TT, E * E]),
                                           ALU.mult))
                steps.wait(v.tensor_tensor(act[:, 0], act[:, 0], act[:, 1], ALU.add))
                steps.wait(v.tensor_reduce(rank[:], cmp_gt, AX.X, ALU.add))
                if layer == 0:
                    ins = v.scalar_tensor_tensor(cw[:], rank[:], TOPK - 0.5, pr[:], ALU.is_lt, ALU.mult)
                else:
                    ins = v.tensor_scalar(cw[:], rank[:], TOPK - 0.5, None, ALU.is_lt)
                steps.wait(ins)
                steps.wait(v.tensor_copy(cw_pair[:, :, 0:E], cw[:]))
                v.tensor_tensor(cw_pair[:, :, E:2 * E], cw[:], cw_pair[:, :, 0:E].bitcast(F32),
                                ALU.subtract).then_inc(cw_made, 1)

            def unit(G, u):
                for half in range(2):
                    n = (G * UNITS + u) * 2 + half
                    if half == 0:
                        ve.wait_ge(cwb_psum, G * UNITS + u + 1)
                    ve.wait_ge(gelu_made, n + 1)
                    v.tensor_tensor(act[:, half], act[:, half], cwb[:], ALU.mult).then_inc(scaled, 1)

            def add(G, layer, c):
                ve.wait_ge(out_psum, G * NC + c + 1)
                xt = panel(xs, G, layer, CT, c * CT).rearrange("p t d -> p (t d)")
                v.tensor_tensor(xt, xt, mix[:, c], ALU.add).then_inc(out_added, 1)

            def run(G, product, experts, layer, e_layer, last=False):
                for what, *n in schedule(product, experts, last, LEAD if product else 0):
                    if what == "tile":
                        tile(G, n[0])
                    elif what == "acc" and e_layer == 1:
                        v.tensor_tensor(xn[:], panel(y_hi, G - 1, 1).bitcast(F32),
                                        panel(y_lo, G - 1, 1).bitcast(F32), ALU.add).then_inc(xn_made, 1)
                    elif what == "own" and e_layer == 1:
                        turned(G - 1, 1, 0)
                    elif what == "graph_out":
                        graph_out(G - 1, e_layer)
                    elif what == "turn":
                        turned(G - 1, e_layer, e_layer)
                    elif what == "gate":
                        gates(G - 1, e_layer)
                    elif what == "unit":
                        unit(G - 1, n[0])
                        if n[0] == E + 2:
                            add(G - 1, e_layer, 0)
                    elif what == "add":
                        add(G - 1, e_layer, n[0])
                    elif what == "next":
                        if n == [0, 0]:
                            ve.wait_ge(a_used, NP * JB)
                        if n[0] == NP - 1 and n[1] == 0:
                            ve.wait_ge(out_added, NP * NC)
                        next_y(NP * NC + n[0] * NC + n[1], n[0] + NP, 1, n[1], False)

            weights(0)
            run(0, True, False, 0, 0)

            def loop(first, layer, per):
                with ve.Fori(first, first + NP - 1) as G:
                    steps.loop(G, first, per, NP - 1)
                    run(G, True, True, layer, layer)
                    steps.end_loop()

            loop(1, 0, STEPS[0])
            run(NP, True, True, 1, 0, last=True)
            weights(1)
            loop(NP + 1, 1, STEPS[1])
            run(2 * NP, False, True, 1, 1)


STEPS = (15, 13)


def program(nc, shapes):
    args = [nc.dram_tensor("in_" + name, shape, F32, kind="ExternalInput").ap() for name, shape in shapes]
    out = nc.dram_tensor("out", (P, JB, D), F32, kind="ExternalOutput").ap()
    two_layers(nc, *args, out)


def kernel(x, adj, L0_gnn_W, L0_ffn_gate_w, L0_ffn_gate_b, L0_ffn_W1, L0_ffn_b1, L0_ffn_W2, L0_ffn_b2,
           L1_gnn_weight, L1_gnn_bias, L1_ffn_Wg, L1_ffn_bg, L1_ffn_W1, L1_ffn_b1, L1_ffn_W2, L1_ffn_b2):
    import concourse.bacc as bacc
    from concourse.bass_utils import run_bass_kernel_spmd

    def lay(a):
        return np.ascontiguousarray(a)

    a = np.asarray(adj)
    weights = []
    for w1, w2 in ((L0_ffn_W1, L0_ffn_W2), (L1_ffn_W1, L1_ffn_W2)):
        w1 = np.asarray(w1).transpose(1, 0, 2).reshape(P, E * H)
        w2 = np.asarray(w2).reshape(E, 2, P, D).transpose(2, 0, 1, 3).reshape(P, E * H)
        weights.append(np.concatenate([w1, w2], 1).reshape(P, WT, PW).transpose(1, 0, 2))
    b1 = [np.asarray(b).reshape(E, 2, P).transpose(2, 0, 1).reshape(P, 2 * E) for b in (L0_ffn_b1, L1_ffn_b1)]
    b2 = [np.concatenate([np.asarray(b)] * 2) for b in (L0_ffn_b2, L1_ffn_b2)]
    gate_b = np.concatenate([np.asarray(L0_ffn_gate_b), np.asarray(L1_ffn_bg)])
    gnn1 = np.asarray(L1_gnn_weight)
    e = np.arange(E)
    arrays = {
        "x": lay(np.asarray(x).reshape(JB, P, D).transpose(1, 0, 2)),
        "adj_rows": lay(a.reshape(JB, P, 8, PW).transpose(0, 2, 1, 3)),
        "adj_cols": lay(a.reshape(NP, PW, JB, P).transpose(0, 2, 3, 1)),
        "w_gnn0": lay(np.asarray(L0_gnn_W).T),
        "w_gnn1_own": lay(gnn1[:D]),
        "w_gnn1_agg": lay(gnn1[D:]),
        "bias_gnn1": lay(np.broadcast_to(np.asarray(L1_gnn_bias), (P, D))),
        "w_experts": lay(np.stack(weights)),
        "b1": lay(np.stack(b1, 1)),
        "b2": lay(np.stack(b2, 1)),
        "w_gate": lay(np.concatenate([np.asarray(L0_ffn_gate_w), np.asarray(L1_ffn_Wg)], 1)),
        "b_gate": lay(np.broadcast_to(gate_b, (P, 2 * E))),
        "ident": np.eye(P, dtype=np.float32),
        "select": np.concatenate([np.eye(E, dtype=np.float32)] * 2),
        "below": lay(np.broadcast_to((e[None, :] < e[:, None]).astype(np.float32).reshape(-1), (P, E * E))),
    }
    nc = bacc.Bacc("TRN2", target_bir_lowering=False, num_devices=1, dynamic_dma_scratch_size=1024)
    program(nc, [(k, v.shape) for k, v in arrays.items()])
    r = run_bass_kernel_spmd(nc, [{"in_" + k: v for k, v in arrays.items()}], core_ids=[0])
    got = r.results[0]["out"]
    return got.transpose(1, 0, 2).reshape(N, D)
```

```python
from contextlib import ExitStack

import numpy as np
import concourse.bass as bass
from concourse import mybir

F32 = mybir.dt.float32
F32R = mybir.dt.float32r
ALU = mybir.AluOpType
ACT = mybir.ActivationFunctionType
AX = mybir.AxisListType

P = 128
N = 8192
D = 128
E = 8
H = 256
TOPK = 2
PW = 1024
NP = N // PW
JB = N // P
TT = PW // P
CH = 512
CT = CH // P
NC = PW // CH
RING = 4
WIDE = 2 * RING
WT = 2 * E * H // PW
UNITS = NC * E
LEAD = 3
LN_EPS = 1e-5
ROW_TILES = NP * TT * 8


def schedule(kind, tiles=JB, lead=0):
    at = {}

    def put(pos, *what):
        at.setdefault(pos, []).append(what)

    def front(s, c):
        put(s - 1, "own_sum", 1, c)
        put(s + 2, "own_turn", 1, c)
        put(s + 4, "graph_out", 1, c)
        put(s + 6, "moments", 1, c)
        put(s + 8, "normalise", 1, c)
        put(s + 10, "turn", 1, c)
        put(s + 12, "gate", 1, c)
        put(s + 14, "softmax", 1, c)
        put(s + 16, "choose", 1, c)
        put(s + 18, "weights_turn", 1, c)

    def units(s, spacing, back, c):
        for e in range(E):
            put(s + spacing * e, "unit", back, c, e)
            put(s + spacing * (e + 1), "second", back, c, e)

    if kind in ("steady", "finish"):
        put(-1, "save", 2, 0)
        put(-1 if kind == "finish" else 1, "add", 2, 0)
    if kind != "first":
        put(-1, "acc", 1, 0)
    if kind == "second":
        front(0, 0)
        front(32, 1)
        units(31, 4, 1, 0)
    if kind == "steady":
        front(0, 0)
        units(-1, 4, 2, 1)
        put(32, "save", 2, 1)
        put(33, "add", 2, 1)
        front(32, 1)
        units(31, 4, 1, 0)
    if kind == "finish":
        front(0, 0)
        front(16, 1)
        units(-1, 2, 2, 1)
        units(19, 2, 1, 0)
        units(37, 2, 1, 1)
        for pos, back, c in ((17, 2, 1), (37, 1, 0), (54, 1, 1)):
            put(pos, "save", back, c)
            put(pos, "add", back, c)
        for i in range(NP * NC) if tiles else ():
            for n, before in ((1, 6), (2, 4), (3, 3)):
                put(55 if i >= (NP - 1) * NC else max(CT * i - 1 - before, -1), f"next{n}", *divmod(i, NC))
    if kind == "first":
        for k, stages in AFTER.items():
            for name, c in stages:
                put(-1 if k == CLOSE else k, name, 0, c)
    for stages in at.values():
        stages.sort(key=lambda w: ORDER.index(w[0]) if w[0] in ORDER else len(ORDER))
    slots = [-1 - -(JB * (k + 1) // tiles) for k in range(tiles)]
    for pos in range(-1, JB + lead):
        for k in range(tiles):
            if slots[k] == pos:
                yield ("tile", JB - tiles + k)
        if pos < JB - 1:
            yield from at.get(pos - (lead if tiles else 0), ())
        elif pos == JB - 1:
            for late in range(pos - (lead if tiles else 0), JB):
                yield from at.get(late, ())


def ahead(tiles):
    return LEAD * JB // max(tiles, 1) if tiles else 0


ORDER = ("unit", "second", "save", "add")

CLOSE = RING - 1
AFTER = {CLOSE: (("close", 0), ("saved", 0)), 7: (("degrees", 0), ("next1", 0)), 15: (("next2", 0),),
         17: (("next_hi", 0),), 23: (("next3", 0), ("next1", 1)), 31: (("next2", 1),), 33: (("next_hi", 1),),
         39: (("next3", 1), ("low_out", 0)), 43: (("low_out", 1),), 47: (("low_add", 0),), 51: (("low_add", 1),)}


def row_pass(p):
    rows = [[("row", t, c) for c in range(p, NP)] for t in range(TT)]
    cols = [[("col", jb) for jb in range(t * p, (t + 1) * p)] for t in range(TT)]
    if p == 1:
        return sum(rows, []) + sum(cols, [])
    return sum((r + c for r, c in zip(rows, cols)), [])


def index(G, jb):
    if isinstance(G, int) and G < NP:
        return LOW + sum(JB - q * TT for q in range(G)) + jb - G * TT
    return G * JB + jb


LOW = sum(p * TT for p in range(NP))


class Steps:

    def __init__(self, eng, sem):
        self.eng, self.sem, self.done, self.shift = eng, sem, 0, None

    def loop(self, var, first, per, times):
        self.shift, self.start, self.per, self.times = (var - first) * per, self.done, per, times

    def end_loop(self):
        assert self.done == self.start + self.per, (self.done - self.start, self.per)
        self.done, self.shift = self.start + self.per * self.times, None

    def wait(self, ins):
        ins.then_inc(self.sem, 1)
        self.done += 1
        self.eng.wait_ge(self.sem, self.done if self.shift is None else self.shift + self.done)


def two_layers(nc, x, adj_rows, adj_cols, w_gnn0, w_gnn1_own, w_gnn1_agg, bias_gnn1, w_experts,
               b1, b2, w_gate, b_gate, ident_in, select_in, below_in, out):
    ctx = ExitStack()
    with ctx:
        def sb(name, shape, dt=F32):
            return ctx.enter_context(nc.sbuf_tensor(name, shape, dt))

        def sem(name):
            return ctx.enter_context(nc.semaphore(name))

        xs = sb("xs", [P, JB, D])
        y_hi = sb("y_hi", [P, JB, D], F32R)
        y_lo = sb("y_lo", [P, JB, D], F32R)
        raw = sb("raw", [P, RING, PW])
        a_hi = sb("a_hi", [P, RING, PW], F32R)
        a_lo = sb("a_lo", [P, RING, PW], F32R)
        with nc.sbuf_tensor("early", [P, WIDE - RING, PW], F32) as early:
            pass
        w_hi = sb("w_hi", [P, WT, PW], F32R)
        w_lo = sb("w_lo", [P, WT, PW], F32R)
        xn = sb("xn", [P, TT, D])
        xt_hi = sb("xt_hi", [P, NC, CH], F32R)
        xt_lo = sb("xt_lo", [P, NC, CH], F32R)
        act = sb("act", [P, 2, CH])
        g_hi = sb("g_hi", [P, 2, CH], F32R)
        g_lo = sb("g_lo", [P, 2, CH], F32R)
        acc_s = sb("acc_s", [P, NC, CH])
        cmp_gt = sb("cmp_gt", [P, CT, E, E])
        cmp_eq = sb("cmp_eq", [P, CT, E, E])
        turn = sb("turn", [P, CT, D])
        cw_t = sb("cw_t", [2 * E, NC, CH], F32R)
        wg0 = sb("wg0", [P, D])
        wg1_agg = sb("wg1_agg", [P, D])
        wg1_own_hi = sb("wg1_own_hi", [P, D], F32R)
        wg1_own_lo = sb("wg1_own_lo", [P, D], F32R)
        bias1 = sb("bias1", [P, D])
        ident = sb("ident", [P, P])
        gate = sb("gate", [P, 2 * E])
        gate_hi = sb("gate_hi", [P, 2 * E], F32R)
        gate_lo = sb("gate_lo", [P, 2 * E], F32R)
        gate_b = sb("gate_b", [P, 2 * E])
        eb1 = sb("eb1", [P, 2, 2 * E])
        eb2_hi = sb("eb2_hi", [2 * E, 2, D], F32R)
        eb2_lo = sb("eb2_lo", [2 * E, 2, D], F32R)
        ones = sb("ones", [P, 1], F32R)
        select = sb("select", [2 * E, E])
        select_r = sb("select_r", [2 * E, E], F32R)
        below = sb("below", [P, E * E])
        sums = sb("sums", [P, 2, TT, 8])
        d_is = sb("d_is", [P, JB])
        deg = sb("deg", [P, TT])
        stats = sb("stats", [P, CT, 6])
        mv = sb("mv", [P, CT, 2])
        rstd = sb("rstd", [P, CT])
        n_stats = sb("n_stats", [P, CT, 6])
        n_mv = sb("n_mv", [P, CT, 2])
        n_rstd = sb("n_rstd", [P, CT])
        pad = sb("pad", [P, 1])
        minus_half = sb("minus_half", [P, TT])
        lg = sb("lg", [P, CT, E])
        pr = sb("pr", [P, CT, E])
        top = sb("top", [P, CT])
        inv = sb("inv", [P, CT])
        rank = sb("rank", [P, CT, E])
        cw = sb("cw", [P, CT, E])
        cw_pair = sb("cw_pair", [P, CT, 2 * E], F32R)
        wg1_own = act[:, 0, 0:D]
        eb2 = act[0:2 * E, 1, 0:2 * D].rearrange("p (l d) -> p l d", l=2)

        acc = ctx.enter_context(nc.psum_tensor("acc", [P, NC, CH], F32))
        hid = ctx.enter_context(nc.psum_tensor("hid", [P, 2, CH], F32))
        cwb = ctx.enter_context(nc.psum_tensor("cwb", [P, CH], F32))
        yps = ctx.enter_context(nc.psum_tensor("yps", [P, CH], F32))
        mix = ctx.enter_context(nc.psum_tensor("mix", [P, NC, CH], F32))

        consts_in = sem("consts_in")
        x_in = sem("x_in")
        landed = [sem(f"landed{i}") for i in range(WIDE)]
        consts_hi = sem("consts_hi")
        consts_lo = sem("consts_lo")
        row_sum_act = sem("row_sum_act")
        row_sum_dve = sem("row_sum_dve")
        w_hi_made = sem("w_hi_made")
        w_lo_made = sem("w_lo_made")
        a_hi_made = sem("a_hi_made")
        a_lo_made = sem("a_lo_made")
        a_used = sem("a_used")
        y_made = sem("y_made")
        y_hi_made = sem("y_hi_made")
        y_lo_made = sem("y_lo_made")
        acc_saved = sem("acc_saved")
        xn_made = sem("xn_made")
        xt_psum = sem("xt_psum")
        xt_hi_made = sem("xt_hi_made")
        xt_lo_made = sem("xt_lo_made")
        graph_psum = sem("graph_psum")
        low_added = sem("low_added")
        gate_psum = sem("gate_psum")
        gate_read = sem("gate_read")
        logits_made = sem("logits_made")
        exp_made = sem("exp_made")
        cw_made = sem("cw_made")
        cwt_psum = sem("cwt_psum")
        cwt_made = sem("cwt_made")
        cwb_psum = sem("cwb_psum")
        hid_psum = sem("hid_psum")
        gelu_made = sem("gelu_made")
        scaled = sem("scaled")
        g_hi_made = sem("g_hi_made")
        g_lo_made = sem("g_lo_made")
        y_done = sem("y_done")
        y_saved = sem("y_saved")
        out_psum = sem("out_psum")
        out_added = sem("out_added")
        compared = sem("compared")
        rank_made = sem("rank_made")
        pool_step = sem("pool_step")
        dve_step = sem("dve_step")
        half_set = sem("half_set")
        deg_made = sem("deg_made")
        deg_rooted = sem("deg_rooted")
        next_var = sem("next_var")
        next_rstd = sem("next_rstd")
        token_var = sem("token_var")
        token_rstd = sem("token_rstd")
        stored = sem("stored")

        consts = [(wg0, w_gnn0), (wg1_agg, w_gnn1_agg), (wg1_own, w_gnn1_own), (bias1, bias_gnn1),
                  (ident, ident_in), (gate, w_gate), (gate_b, b_gate), (eb1, b1), (eb2, b2),
                  (select, select_in), (below, below_in)]
        splits = [(wg1_own, wg1_own_hi, wg1_own_lo), (gate, gate_hi, gate_lo), (eb2, eb2_hi, eb2_lo)]

        LATER = NP - 1

        def turns(G, layer, again, c):
            return G * NC + c if layer == 0 else NC * NP + (G - NP) * 2 * NC + 2 * c + again

        def tile_use(G, jb):
            before = ROW_TILES * RING // WIDE + WT - LOW
            return (before + index(G, jb)) // RING if isinstance(G, int) \
                else G * (JB // RING) + (before + jb) // RING

        def panel(t, G, layer, n=TT, first=0):
            if isinstance(G, int):
                a = (G - layer * NP) * TT + first
                return t[:, a:a + n]
            return t[:, bass.ds((G - layer * NP) * TT + first, n)]

        passes = [row_pass(p) for p in range(NP)]
        summed = {}
        for p in range(NP):
            for what, *n in passes[p]:
                if what == "row":
                    k = len(summed)
                    summed[(p, *n)] = (k % 2 == 0, k // 2 + 1)

        def wait_freed(eng, p, item):
            what, *n = item
            if what == "col":
                eng.wait_ge(a_lo_made, index_low(p, n[0]) + 1)
            else:
                by_act, count = summed[(p, *n)]
                eng.wait_ge(row_sum_act if by_act else row_sum_dve, count)

        def wide(k):
            s = k % WIDE
            return raw[:, s] if s < RING else early[:, s - RING]

        def index_low(p, jb):
            return sum(q * TT for q in range(p)) + jb

        block = ctx.enter_context(nc.Block())

        @block.sync
        def _(sp):
            sp.dma_start(xs[:], x).then_inc(x_in, 16)
            for t, src in consts:
                sp.dma_start(t[:], src).then_inc(consts_in, 16)

            for p in range(NP):
                for k, (what, *n) in enumerate(passes[p]):
                    if p or k >= WIDE:
                        before = (p, passes[p][k - WIDE]) if k >= WIDE else (p - 1, passes[p - 1][k - WIDE])
                        wait_freed(sp, *before)
                    src = adj_rows[p * TT + n[0], n[1]] if what == "row" else adj_cols[p, n[0]]
                    sp.dma_start(wide(k), src).then_inc(landed[k % WIDE], 16)

            def weight_tiles(layer):
                for i in range(WT):
                    if layer == 0:
                        wait_freed(sp, NP - 1, passes[NP - 1][i - WIDE])
                    else:
                        sp.wait_ge(a_lo_made, (NP + 1) * JB - RING + i + 1)
                    sp.dma_start(raw[:, i], w_experts[layer, i]).then_inc(landed[i], 16)

            def col_tiles(G, layer, skip=0):
                for jb in range((G * TT if layer == 0 else 0), JB):
                    if jb >= skip:
                        sp.wait_ge(a_lo_made, index(G, jb) - RING + 1)
                    src = adj_cols[G - layer * NP, jb] if isinstance(G, int) else \
                        adj_cols[bass.ds(G - layer * NP, 1), jb].rearrange("o p n -> (o p) n")
                    sp.dma_start(raw[:, jb % RING], src).then_inc(landed[jb % RING], 16)

            weight_tiles(0)
            sp.wait_ge(w_lo_made, WT)
            col_tiles(0, 0, skip=RING)
            for G in range(1, NP):
                col_tiles(G, 0)
            col_tiles(NP, 1)
            weight_tiles(1)
            sp.wait_ge(w_lo_made, 2 * WT)
            with sp.Fori(NP + 1, 2 * NP) as G:
                col_tiles(G, 1)
            for p in range(NP):
                for c in range(NC):
                    sp.wait_ge(out_added, (NP + p) * NC + c + 1)
                    a = p * TT + c * CT
                    sp.dma_start(out[:, a:a + CT], xs[:, a:a + CT]).then_inc(stored, 16)
            sp.wait_ge(stored, 16 * NP * NC)

        @block.tensor
        def _(pe):
            def three(o, l_hi, l_lo, r_hi, r_lo, start, stop):
                pe.matmul(o, l_hi, r_hi, start=start, stop=False)
                pe.matmul(o, l_hi, r_lo, start=False, stop=False)
                return pe.matmul(o, l_lo, r_hi, start=False, stop=stop)

            def product(jb, first, last):
                s = jb % RING
                for hi_or_lo, left in ((a_hi, y_hi), (a_lo, y_hi), (a_hi, y_lo)):
                    for c in range(NC):
                        mm = pe.matmul(acc[:, c], left[:, jb], hi_or_lo[:, s, c * CH:(c + 1) * CH],
                                       start=(first and hi_or_lo is a_hi and left is y_hi),
                                       stop=(last and left is y_lo))
                mm.then_inc(a_used, 1)

            def low_tile(p, jb):
                if jb == 0 and p > 1:
                    pe.wait_ge(acc_saved, p - 1)
                    pe.wait_ge(deg_made, p)
                if jb % CT == 0:
                    pe.wait_ge(y_lo_made, jb // CT + 1)
                pe.wait_ge(a_lo_made, index_low(p, jb) + 1)
                for part in (a_hi, a_lo):
                    for c in range(NC):
                        pe.matmul(hid[:, c], ones[:].broadcast_to([P, P]), part[:, jb % RING, c * CH:(c + 1) * CH],
                                  start=(jb == 0 and part is a_hi), stop=(jb == p * TT - 1 and part is a_lo))
                product(jb, jb == 0, jb == p * TT - 1)

            def tile(G, layer, jb, first_panel):
                first = jb == (G * TT if layer == 0 else 0)
                if first:
                    pe.wait_ge(acc_saved, G + LATER)
                if first_panel and jb % CT == 0:
                    pe.wait_ge(y_lo_made, layer * NP * NC + jb // CT + 1)
                pe.wait_ge(a_lo_made, index(G, jb) + 1)
                product(jb, first, jb == JB - 1)

            def low_out(n, c):
                pe.wait_ge(acc_saved, n + 1)
                if n > 0:
                    pe.wait_ge(low_added, (n - 1) * NC + c + 1)
                for t in range(CT):
                    mm = pe.matmul(mix[:, c, t * P:(t + 1) * P], acc_s[:, c, t * P:(t + 1) * P], wg0[:],
                                   start=True, stop=True)
                mm.then_inc(graph_psum, 1)

            def bank_free(G, c):
                if isinstance(G, int) and G == 0:
                    pe.wait_ge(low_added, (LATER - 1) * NC + c + 1)
                else:
                    pe.wait_ge(out_added, (G - 1) * NC + c + 1)

            def turn_chunk(G, layer, again, c):
                if layer == 1 and not again:
                    bank_free(G, c)
                pe.wait_ge(xn_made, turns(G, layer, again, c) + 1)
                for t in range(CT):
                    mm = pe.transpose(mix[:, c, t * P:(t + 1) * P], xn[:, c * CT + t], ident[:])
                mm.then_inc(xt_psum, 1)

            def graph_out(G, layer, c):
                pe.wait_ge(acc_saved, G + 1 + LATER)
                if layer == 0:
                    bank_free(G, c)
                if layer == 1:
                    pe.wait_ge(xt_lo_made, turns(G, 1, 0, c) + 1)
                for t in range(CT):
                    o = mix[:, c, t * P:(t + 1) * P]
                    col = slice(t * P, (t + 1) * P)
                    if layer == 1:
                        pe.matmul(o, xt_hi[:, c, col], wg1_own_hi[:], start=True, stop=False)
                        pe.matmul(o, xt_hi[:, c, col], wg1_own_lo[:], start=False, stop=False)
                        pe.matmul(o, xt_lo[:, c, col], wg1_own_hi[:], start=False, stop=False)
                    mm = pe.matmul(o, acc_s[:, c, col], (wg1_agg if layer else wg0)[:],
                                   start=(layer == 0), stop=True)
                mm.then_inc(graph_psum, 1)

            def gates(G, layer, c):
                pe.wait_ge(xt_lo_made, turns(G, layer, layer, c) + 1)
                ge = slice(layer * E, (layer + 1) * E)
                for t in range(CT):
                    col = slice(t * P, (t + 1) * P)
                    mm = three(mix[:, c, t * E:(t + 1) * E], xt_hi[:, c, col], xt_lo[:, c, col],
                               gate_hi[:, ge], gate_lo[:, ge], True, True)
                mm.then_inc(gate_psum, 1)

            def weights_turn(G, c):
                pe.wait_ge(cw_made, G * NC + c + 1)
                for t in range(CT):
                    mm = pe.transpose(mix[0:2 * E, c, t * P:(t + 1) * P], cw_pair[:, t].bitcast(F32), ident[:])
                mm.then_inc(cwt_psum, 1)

            def unit(G, layer, c, e):
                u = G * UNITS + c * E + e
                if e == 0:
                    pe.wait_ge(cwt_made, G * NC + c + 1)
                if not (isinstance(G, int) and G == 0 and c + e == 0):
                    pe.wait_ge(scaled, u * 2)
                pe.matmul(cwb[:], select_r[:, e:e + 1].broadcast_to([2 * E, P]), cw_t[:, c],
                          start=True, stop=True).then_inc(cwb_psum, 1)
                for half in range(2):
                    if not (isinstance(G, int) and G == 0 and c + e == 0):
                        pe.wait_ge(gelu_made, (u - 1) * 2 + half + 1)
                    col = e * H + half * P
                    three(hid[:, half], w_hi[:, col // PW, col % PW:col % PW + P],
                          w_lo[:, col // PW, col % PW:col % PW + P], xt_hi[:, c], xt_lo[:, c],
                          True, True).then_inc(hid_psum, 1)

            def second(G, layer, c, e):
                if e == 0:
                    if not (isinstance(G, int) and G == 0 and c == 0):
                        pe.wait_ge(y_saved, G * NC + c)
                    pe.matmul(yps[:], eb2_hi[:, layer], cw_t[:, c], start=True, stop=False)
                    pe.matmul(yps[:], eb2_lo[:, layer], cw_t[:, c], start=False, stop=False)
                for half in range(2):
                    v = (G * UNITS + c * E + e) * 2 + half
                    col = (e * 2 + half) * D
                    l_hi = w_hi[:, WT // 2 + col // PW, col % PW:col % PW + D]
                    l_lo = w_lo[:, WT // 2 + col // PW, col % PW:col % PW + D]
                    pe.wait_ge(g_hi_made, v + 1)
                    pe.matmul(yps[:], l_hi, g_hi[:, half], start=False, stop=False)
                    pe.matmul(yps[:], l_lo, g_hi[:, half], start=False, stop=False)
                    pe.wait_ge(g_lo_made, v + 1)
                    pe.matmul(yps[:], l_hi, g_lo[:, half], start=False,
                              stop=(e == E - 1 and half == 1)).then_inc(y_done, 1)

            def add(G, c):
                pe.wait_ge(y_saved, G * NC + c + 1)
                for t in range(CT):
                    mm = pe.transpose(mix[:, c, t * P:(t + 1) * P], turn[:, t], ident[:])
                mm.then_inc(out_psum, 1)

            def run(G, kind, layer, e_layer, tiles=JB, first_panel=False):
                for what, *n in schedule(kind, tiles):
                    if what == "tile":
                        tile(G, layer, n[0], first_panel)
                        continue
                    back, c, *e = n
                    if what == "low_out":
                        low_out(LATER - 1, c)
                    if what == "own_turn" and e_layer == 1:
                        turn_chunk(G - back, 1, 0, c)
                    elif what == "graph_out":
                        graph_out(G - back, e_layer, c)
                    elif what == "turn":
                        turn_chunk(G - back, e_layer, e_layer, c)
                    elif what == "gate":
                        gates(G - back, e_layer, c)
                    elif what == "weights_turn":
                        weights_turn(G - back, c)
                    elif what == "unit":
                        unit(G - back, e_layer, c, *e)
                    elif what == "second":
                        second(G - back, e_layer, c, *e)
                    elif what == "add":
                        add(G - back, c)

            pe.wait_ge(consts_lo, 1)
            for p in range(NP):
                for k, (what, *n) in enumerate(passes[p]):
                    if what == "col":
                        low_tile(p, n[0])
                    for stage, c in AFTER.get(k, ()) if p > 1 else ():
                        if stage == "low_out":
                            low_out(p - 2, c)
            run(0, "first", 0, 0, first_panel=True)
            run(1, "second", 0, 0, JB - TT)
            for G in range(2, NP):
                run(G, "steady", 0, 0, JB - G * TT)
            run(NP, "finish", 1, 0, first_panel=True)
            pe.wait_ge(w_lo_made, 2 * WT)
            run(NP + 1, "second", 1, 1)
            with pe.Fori(NP + 2, 2 * NP) as G:
                run(G, "steady", 1, 1)
            run(2 * NP, "finish", 1, 1, tiles=0)

        @block.scalar
        def _(sc):
            def copy(o, i):
                return nc.scalar.activation(o, i, ACT.Copy)

            sc.wait_ge(consts_in, 16 * len(consts))
            copy(select_r[:], select[:])
            for full, hi, _ in splits:
                ins = copy(hi[:], full[:])
            ins.then_inc(consts_hi, 1)

            def next_y(count, p, layer, half):
                sc.wait_ge(y_made, count + 1)
                if isinstance(p, int) and p == NP and half == 0:
                    sc.wait_ge(a_used, NP * JB)
                copy(panel(y_hi, p, layer, CT, half * CT), turn[:]).then_inc(y_hi_made, 1)

            def save_low(n):
                sc.wait_ge(a_used, sum(q * TT for q in range(n + 2)))
                if n > 0:
                    sc.wait_ge(graph_psum, n * NC)
                copy(acc_s[:], acc[:]).then_inc(acc_saved, 1)

            def high(full, s, use, at, used):
                sc.wait_ge(landed[s], (use + 1) * 16)
                if used is not None:
                    sc.wait_ge(a_used, used)
                copy(a_hi[:, at], full).then_inc(a_hi_made, 1)

            for p in range(NP):
                for k, (what, *n) in enumerate(passes[p]):
                    s, use = k % WIDE, (p * JB + k) // WIDE
                    if what == "col":
                        i = index_low(p, n[0])
                        high(wide(k), s, use, i % RING, i - RING + 1 if i >= RING else None)
                    elif summed[(p, *n)][0]:
                        if n[0] == 0 and p > 1:
                            sc.wait_ge(deg_made, p - 1)
                        sc.wait_ge(landed[s], (use + 1) * 16)
                        nc.scalar.activation(wide(k), wide(k), ACT.Copy,
                                             accum_out=sums[:, p % 2, n[0], n[1]:n[1] + 1]).then_inc(row_sum_act, 1)
                    for stage, half in AFTER.get(k, ()):
                        if stage == "saved" and p > 1:
                            save_low(p - 2)
                        elif stage == "next_hi" and p > 0:
                            next_y((p - 1) * NC + half, p - 1, 0, half)

            def weights(layer):
                for i in range(WT):
                    n = ROW_TILES // WIDE if layer == 0 else tile_use(NP + 1, 0)
                    if layer == 0 and i == 0:
                        sc.wait_ge(a_lo_made, LOW)
                        sc.wait_ge(row_sum_dve, len(summed) // 2)
                    sc.wait_ge(landed[i], (n + 1) * 16)
                    copy(w_hi[:, i], raw[:, i]).then_inc(w_hi_made, 1)

            def tile(G, jb, shift):
                high(raw[:, jb % RING], jb % RING, tile_use(G, jb) + shift, jb % RING, index(G, jb) - RING + 1)

            def turned(G, layer, again, c):
                sc.wait_ge(xt_psum, turns(G, layer, again, c) + 1)
                copy(xt_hi[:, c], mix[:, c]).then_inc(xt_hi_made, 1)

            def unit(G, layer, c, e):
                start = isinstance(G, int) and G == 0 and c + e == 0
                for half in range(2):
                    v = (G * UNITS + c * E + e) * 2 + half
                    sc.wait_ge(hid_psum, v + 1)
                    if not start:
                        sc.wait_ge(g_lo_made, v - 1)
                    b = (layer, e * 2 + half)
                    nc.scalar.activation(act[:, half], hid[:, half], ACT.Gelu,
                                         bias=eb1[:, b[0], b[1]:b[1] + 1]).then_inc(gelu_made, 1)
                for half in range(2):
                    v = (G * UNITS + c * E + e) * 2 + half
                    sc.wait_ge(scaled, v + 1)
                    if not start:
                        sc.wait_ge(y_done, v - 1)
                    copy(g_hi[:, half], act[:, half]).then_inc(g_hi_made, 1)

            def save(G, c, nexts):
                sc.wait_ge(y_done, (G * UNITS + (c + 1) * E) * 2)
                if nexts is not None:
                    sc.wait_ge(y_lo_made, nexts)
                if not (isinstance(G, int) and G == 0 and c == 0):
                    sc.wait_ge(out_psum, G * NC + c)
                copy(turn[:].rearrange("p t d -> p (t d)"), yps[:]).then_inc(y_saved, 1)

            def run(G, kind, layer, e_layer, tiles=JB, shift=0):
                nexts = NP * NC if kind == "finish" and tiles else None
                for what, *n in schedule(kind, tiles, ahead(tiles)):
                    if what == "tile":
                        tile(G, n[0], shift)
                        continue
                    back, c, *e = n
                    if what == "acc":
                        sc.wait_ge(a_used, index(G - 1, JB - 1) + 1)
                        if isinstance(G, int) and G == 1:
                            sc.wait_ge(graph_psum, LATER * NC)
                        copy(acc_s[:], acc[:]).then_inc(acc_saved, 1)
                    elif what == "own_turn" and e_layer == 1:
                        turned(G - back, 1, 0, c)
                    elif what == "turn":
                        turned(G - back, e_layer, e_layer, c)
                    elif what == "gate" and e_layer == 0:
                        q = (G - back) * NC + c
                        sc.wait_ge(logits_made, q + 1)
                        nc.scalar.activation(pr[:], lg[:], ACT.Exp).then_inc(exp_made, 1)
                    elif what == "weights_turn":
                        q = (G - back) * NC + c
                        sc.wait_ge(cwt_psum, q + 1)
                        copy(cw_t[:, c], mix[0:2 * E, c]).then_inc(cwt_made, 1)
                    elif what == "unit":
                        unit(G - back, e_layer, c, *e)
                    elif what == "save":
                        save(G - back, c, nexts)
                    elif what == "next2" and kind == "finish":
                        next_y(nexts, back + NP, 1, c)
                        nexts += 1
                    elif what == "next_hi":
                        next_y((NP - 1) * NC + c, NP - 1, 0, c)
                    elif what == "saved":
                        save_low(LATER - 1)

            weights(0)
            run(0, "first", 0, 0)
            run(1, "second", 0, 0, JB - TT)
            for G in range(2, NP):
                run(G, "steady", 0, 0, JB - G * TT)
            run(NP, "finish", 1, 0)
            weights(1)
            run(NP + 1, "second", 1, 1, shift=WT // RING)
            with sc.Fori(NP + 2, 2 * NP) as G:
                run(G, "steady", 1, 1, shift=WT // RING)
            run(2 * NP, "finish", 1, 1, tiles=0)

        @block.gpsimd
        def _(pool):
            def root(t, n, made, done, count):
                pool.wait_ge(made, count + 1)
                nc.gpsimd.tensor_tensor(t[:, 0:n], t[:, 0:n], minus_half[:, 0:n], ALU.pow).then_inc(done, 1)

            def rows_of(p):
                root(deg, TT, deg_made, deg_rooted, p)
                for half in range(NC):
                    root(n_rstd, CT, next_var, next_rstd, p * NC + half)

            def rank_of(q):
                pool.wait_ge(compared, q + 1)
                eq = cmp_eq[:].rearrange("p t a b -> p t (a b)")
                nc.gpsimd.tensor_tensor(eq, eq, below[:].unsqueeze(1).broadcast_to([P, CT, E * E]),
                                        ALU.mult).then_inc(pool_step, 1)
                pool.wait_ge(pool_step, q + 1)
                nc.gpsimd.tensor_tensor(cmp_gt[:], cmp_gt[:], cmp_eq[:], ALU.add).then_inc(rank_made, 1)

            def unit(G, c, e):
                for half in range(2):
                    pool.wait_ge(g_hi_made, (G * UNITS + c * E + e) * 2 + half + 1)
                    nc.gpsimd.tensor_tensor(g_lo[:, half], act[:, half], g_hi[:, half].bitcast(F32),
                                            ALU.subtract).then_inc(g_lo_made, 1)

            def next_low(i):
                pool.wait_ge(y_hi_made, NP * NC + i + 1)
                y = slice(i * CT, (i + 1) * CT)
                nc.gpsimd.tensor_tensor(y_lo[:, y], turn[:], y_hi[:, y].bitcast(F32),
                                        ALU.subtract).then_inc(y_lo_made, 1)

            def run(G, kind, tiles=JB):
                for what, *n in schedule(kind, tiles, ahead(tiles)):
                    if what == "tile":
                        continue
                    back, c, *e = n
                    if what == "moments":
                        root(rstd, CT, token_var, token_rstd, (G - back) * NC + c)
                    elif what == "softmax":
                        rank_of((G - back) * NC + c)
                    elif what == "unit":
                        unit(G - back, c, *e)
                    elif what == "next3" and kind == "finish":
                        next_low(back * NC + c)
                    elif what == "next1" and kind == "finish":
                        root(n_rstd, CT, next_var, next_rstd, NP * NC + back * NC + c)

            nc.gpsimd.memset(minus_half[:], -0.5).then_inc(half_set, 1)
            pool.wait_ge(half_set, 1)
            with pool.Fori(0, NP) as p:
                rows_of(p)
            run(1, "second", JB - TT)
            for G in range(2, NP):
                run(G, "steady", JB - G * TT)
            run(NP, "finish")
            run(NP + 1, "second")
            with pool.Fori(NP + 2, 2 * NP) as G:
                run(G, "steady")
            run(2 * NP, "finish", tiles=0)

        @block.vector
        def _(ve):
            v = nc.vector
            steps = Steps(ve, dve_step)

            steps.wait(v.memset(ones[:].bitcast(F32), 1.0))
            ve.wait_ge(consts_hi, 1)
            for full, hi, lo in splits:
                ins = v.tensor_tensor(lo[:], full[:], hi[:].bitcast(F32), ALU.subtract)
            ins.then_inc(consts_lo, 1)
            ve.wait_ge(x_in, 16)

            def moments(p, layer, first, n, st, m, r, var_sem):
                v.memset(pad[:], 0.0)
                for t in range(n):
                    ins = v.bn_stats(st[:, t], panel(xs, p, layer, 1, first + t).rearrange("p o d -> p (o d)"))
                steps.wait(ins)
                v.memset(pad[:], 0.0)
                for t in range(n):
                    ins = v.bn_aggr(m[:, t], st[:, t])
                steps.wait(ins)
                v.tensor_scalar(r[:, 0:n], m[:, 0:n, 1], LN_EPS, None, ALU.add).then_inc(var_sem, 1)

            def next1(p, layer, half):
                moments(p, layer, half * CT, CT, n_stats, n_mv, n_rstd, next_var)

            def next2(count, p, layer, half, scale):
                ve.wait_ge(next_rstd, count + 1)
                if count > 0:
                    ve.wait_ge(y_lo_made, count)
                if scale:
                    steps.wait(v.tensor_tensor(n_rstd[:], n_rstd[:],
                                               (d_is[:, half * CT + p * TT:half * CT + p * TT + CT] if isinstance(p, int)
                                                else d_is[:, bass.ds(p * TT + half * CT, CT)]), ALU.mult))
                for t in range(CT):
                    ins = v.tensor_scalar(turn[:, t], panel(xs, p, layer, 1, half * CT + t).rearrange("p o d -> p (o d)"),
                                          n_mv[:, t, 0:1], n_rstd[:, t:t + 1], ALU.subtract, ALU.mult)
                ins.then_inc(y_made, 1)

            def next3(count, p, layer, half):
                ve.wait_ge(y_hi_made, count + 1)
                v.tensor_tensor(panel(y_lo, p, layer, CT, half * CT), turn[:],
                                panel(y_hi, p, layer, CT, half * CT).bitcast(F32),
                                ALU.subtract).then_inc(y_lo_made, 1)

            def degrees(p):
                ve.wait_ge(deg_rooted, p + 1)
                scale = d_is[:, p * TT:(p + 1) * TT] if isinstance(p, int) else d_is[:, bass.ds(p * TT, TT)]
                steps.wait(v.tensor_copy(scale, deg[:]))

            def low(full, at, i):
                ve.wait_ge(a_hi_made, i + 1)
                v.tensor_tensor(a_lo[:, at], full, a_hi[:, at].bitcast(F32),
                                ALU.subtract).then_inc(a_lo_made, 1)

            def close(p):
                for mine, done in ((True, row_sum_act), (False, row_sum_dve)):
                    ve.wait_ge(done, max(n for q, (by_act, n) in summed.items() if by_act == mine and q[0] <= p))
                if p > 0:
                    ve.wait_ge(a_used, index_low(p + 1, 0))
                    diag = act[:].rearrange("p c (t n) -> p (c t) n", n=P)
                    steps.wait(v.tensor_tensor(diag, hid[:].rearrange("p c (t n) -> p (c t) n", n=P),
                                               ident[:].unsqueeze(1).broadcast_to([P, TT, P]), ALU.mult))
                    steps.wait(v.tensor_reduce(sums[:, p % 2, :, p - 1], diag, AX.X, ALU.add))
                v.tensor_reduce(deg[:], sums[:, p % 2, :, max(p - 1, 0):], AX.X, ALU.add).then_inc(deg_made, 1)

            def low_out(p, c):
                add_rows(p, c, (p - 1) * NC + c)
                ins = v.memset(pad[:], 0.0)
                ins.then_inc(low_added, 1)

            def add_rows(G, c, count):
                ve.wait_ge(graph_psum, count + 1)
                for t in range(CT):
                    xt = xs[:, G * TT + c * CT + t]
                    col = G * TT + c * CT + t
                    ins = v.scalar_tensor_tensor(xt, mix[:, c, t * P:(t + 1) * P], d_is[:, col:col + 1], xt,
                                                 ALU.mult, ALU.add)
                steps.wait(ins)

            def after(stage, p, half):
                if stage == "degrees":
                    degrees(p)
                elif stage == "next1":
                    next1(p, 0, half)
                elif stage == "next2":
                    next2(p * NC + half, p, 0, half, True)
                elif stage == "next3":
                    next3(p * NC + half, p, 0, half)
                elif stage == "close":
                    close(p)
                elif stage == "low_add" and p > 0:
                    low_out(p, half)

            for p in range(NP):
                for k, (what, *n) in enumerate(passes[p]):
                    s, use = k % WIDE, (p * JB + k) // WIDE
                    if what == "col":
                        low(wide(k), n[0] % RING, index_low(p, n[0]))
                    elif not summed[(p, *n)][0]:
                        ve.wait_ge(landed[s], (use + 1) * 16)
                        v.tensor_reduce(sums[:, p % 2, n[0], n[1]:n[1] + 1], wide(k), AX.X,
                                        ALU.add).then_inc(row_sum_dve, 1)
                    for stage, half in AFTER.get(k, ()) if p > 0 else ():
                        after(stage, p - 1, half)

            def weights(layer):
                for i in range(WT):
                    ve.wait_ge(w_hi_made, layer * WT + i + 1)
                    v.tensor_tensor(w_lo[:, i], raw[:, i], w_hi[:, i].bitcast(F32),
                                    ALU.subtract).then_inc(w_lo_made, 1)

            def tile(G, jb):
                low(raw[:, jb % RING], jb % RING, index(G, jb))

            def turned(G, layer, again, c):
                ve.wait_ge(xt_hi_made, turns(G, layer, again, c) + 1)
                v.tensor_tensor(xt_lo[:, c], mix[:, c], xt_hi[:, c].bitcast(F32),
                                ALU.subtract).then_inc(xt_lo_made, 1)

            def own_sum(G, c):
                v.tensor_tensor(xn[:, c * CT:(c + 1) * CT], panel(y_hi, G, 1, CT, c * CT).bitcast(F32),
                                panel(y_lo, G, 1, CT, c * CT).bitcast(F32), ALU.add).then_inc(xn_made, 1)

            def graph_out(G, layer, c):
                if layer == 0:
                    add_rows(G, c, (LATER + G) * NC + c)
                    return
                ve.wait_ge(graph_psum, (LATER + G) * NC + c + 1)
                for t in range(CT):
                    m = mix[:, c, t * P:(t + 1) * P]
                    ins = v.tensor_tensor(m, m, bias1[:], ALU.add)
                steps.wait(ins)
                xt = panel(xs, G, 1, CT, c * CT).rearrange("p t d -> p (t d)")
                steps.wait(v.scalar_tensor_tensor(xt, mix[:, c], 0.0, xt, ALU.max, ALU.add))

            def normalise(G, layer, c):
                ve.wait_ge(token_rstd, G * NC + c + 1)
                for t in range(CT):
                    ins = v.tensor_scalar(xn[:, c * CT + t],
                                          panel(xs, G, layer, 1, c * CT + t).rearrange("p o d -> p (o d)"),
                                          mv[:, t, 0:1], rstd[:, t:t + 1], ALU.subtract, ALU.mult)
                ins.then_inc(xn_made, 1)

            def gates(G, layer, c):
                ve.wait_ge(gate_psum, G * NC + c + 1)
                bg = gate_b[:, layer * E:(layer + 1) * E].unsqueeze(1).broadcast_to([P, CT, E])
                steps.wait(v.tensor_tensor(lg[:], mix[:, c, 0:CT * E].rearrange("p (t e) -> p t e", e=E),
                                           bg, ALU.add))
                if layer == 0:
                    steps.wait(v.tensor_reduce(top[:], lg[:], AX.X, ALU.max))
                    v.tensor_tensor(lg[:], lg[:], top[:].unsqueeze(2).broadcast_to([P, CT, E]),
                                    ALU.subtract).then_inc(logits_made, 1)

            def softmax(G, c):
                ve.wait_ge(exp_made, G * NC + c + 1)
                steps.wait(v.tensor_reduce(top[:], pr[:], AX.X, ALU.add))
                steps.wait(v.reciprocal(inv[:], top[:]))
                steps.wait(v.tensor_tensor(pr[:], pr[:], inv[:].unsqueeze(2).broadcast_to([P, CT, E]),
                                           ALU.mult))

            def compare(score):
                other = score[:].unsqueeze(2).broadcast_to([P, CT, E, E])
                own = score[:].unsqueeze(3).broadcast_to([P, CT, E, E])
                steps.wait(v.tensor_tensor(cmp_gt[:], other, own, ALU.is_gt))
                v.tensor_tensor(cmp_eq[:], other, own, ALU.is_equal).then_inc(compared, 1)

            def choose(G, layer, c):
                ve.wait_ge(rank_made, G * NC + c + 1)
                steps.wait(v.tensor_reduce(rank[:], cmp_gt[:], AX.X, ALU.add))
                if layer == 0:
                    ins = v.scalar_tensor_tensor(cw[:], rank[:], TOPK - 0.5, pr[:], ALU.is_lt, ALU.mult)
                else:
                    ins = v.tensor_scalar(cw[:], rank[:], TOPK - 0.5, None, ALU.is_lt)
                steps.wait(ins)
                steps.wait(v.tensor_copy(cw_pair[:, :, 0:E], cw[:]))
                v.tensor_tensor(cw_pair[:, :, E:2 * E], cw[:], cw_pair[:, :, 0:E].bitcast(F32),
                                ALU.subtract).then_inc(cw_made, 1)

            def unit(G, c, e):
                u = G * UNITS + c * E + e
                for half in range(2):
                    if half == 0:
                        ve.wait_ge(cwb_psum, u + 1)
                    ve.wait_ge(gelu_made, 2 * u + half + 1)
                    v.tensor_tensor(act[:, half], act[:, half], cwb[:], ALU.mult).then_inc(scaled, 1)

            def add(G, layer, c):
                ve.wait_ge(out_psum, G * NC + c + 1)
                xt = panel(xs, G, layer, CT, c * CT).rearrange("p t d -> p (t d)")
                v.tensor_tensor(xt, xt, mix[:, c], ALU.add).then_inc(out_added, 1)

            def run(G, kind, layer, e_layer, tiles=JB):
                for what, *n in schedule(kind, tiles, ahead(tiles)):
                    if what == "tile":
                        tile(G, n[0])
                        continue
                    back, c, *e = n
                    if what == "own_sum" and e_layer == 1:
                        own_sum(G - back, c)
                    elif what == "own_turn" and e_layer == 1:
                        turned(G - back, 1, 0, c)
                    elif what == "graph_out":
                        graph_out(G - back, e_layer, c)
                    elif what == "moments":
                        moments(G - back, e_layer, c * CT, CT, stats, mv, rstd, token_var)
                    elif what == "normalise":
                        normalise(G - back, e_layer, c)
                    elif what == "turn":
                        turned(G - back, e_layer, e_layer, c)
                    elif what == "gate":
                        gates(G - back, e_layer, c)
                    elif what == "softmax":
                        if e_layer == 0:
                            softmax(G - back, c)
                        compare(lg if e_layer else pr)
                    elif what == "choose":
                        choose(G - back, e_layer, c)
                    elif what == "unit":
                        unit(G - back, c, *e)
                    elif what == "add":
                        add(G - back, e_layer, c)
                    elif kind == "first":
                        after(what, NP - 1, c)
                    elif what == "next1":
                        if back == NP - 1 and c == 0:
                            ve.wait_ge(out_added, NP * NC)
                        next1(NP + back, 1, c)
                    elif what == "next2":
                        next2((NP + back) * NC + c, NP + back, 1, c, False)

            def loop(first, layer):
                with ve.Fori(first, first + NP - 2) as G:
                    steps.loop(G, first, STEPS, NP - 2)
                    run(G, "steady", layer, layer)
                    steps.end_loop()

            weights(0)
            run(0, "first", 0, 0)
            run(1, "second", 0, 0, JB - TT)
            for G in range(2, NP):
                run(G, "steady", 0, 0, JB - G * TT)
            run(NP, "finish", 1, 0)
            weights(1)
            run(NP + 1, "second", 1, 1)
            loop(NP + 2, 1)
            run(2 * NP, "finish", 1, 1, tiles=0)


STEPS = 18


def program(nc, shapes):
    args = [nc.dram_tensor("in_" + name, shape, F32, kind="ExternalInput").ap() for name, shape in shapes]
    out = nc.dram_tensor("out", (P, JB, D), F32, kind="ExternalOutput").ap()
    two_layers(nc, *args, out)


def kernel(x, adj, L0_gnn_W, L0_ffn_gate_w, L0_ffn_gate_b, L0_ffn_W1, L0_ffn_b1, L0_ffn_W2, L0_ffn_b2,
           L1_gnn_weight, L1_gnn_bias, L1_ffn_Wg, L1_ffn_bg, L1_ffn_W1, L1_ffn_b1, L1_ffn_W2, L1_ffn_b2):
    import concourse.bacc as bacc
    from concourse.bass_utils import run_bass_kernel_spmd

    def lay(a):
        return np.ascontiguousarray(a)

    a = np.asarray(adj)
    weights = []
    for w1, w2 in ((L0_ffn_W1, L0_ffn_W2), (L1_ffn_W1, L1_ffn_W2)):
        w1 = np.asarray(w1).transpose(1, 0, 2).reshape(P, E * H)
        w2 = np.asarray(w2).reshape(E, 2, P, D).transpose(2, 0, 1, 3).reshape(P, E * H)
        weights.append(np.concatenate([w1, w2], 1).reshape(P, WT, PW).transpose(1, 0, 2))
    b1 = [np.asarray(b).reshape(E, 2, P).transpose(2, 0, 1).reshape(P, 2 * E) for b in (L0_ffn_b1, L1_ffn_b1)]
    b2 = [np.concatenate([np.asarray(b)] * 2) for b in (L0_ffn_b2, L1_ffn_b2)]
    gate_b = np.concatenate([np.asarray(L0_ffn_gate_b), np.asarray(L1_ffn_bg)])
    gnn1 = np.asarray(L1_gnn_weight)
    e = np.arange(E)
    arrays = {
        "x": lay(np.asarray(x).reshape(JB, P, D).transpose(1, 0, 2)),
        "adj_rows": lay(a.reshape(JB, P, 8, PW).transpose(0, 2, 1, 3)),
        "adj_cols": lay(a.reshape(NP, PW, JB, P).transpose(0, 2, 3, 1)),
        "w_gnn0": lay(np.asarray(L0_gnn_W).T),
        "w_gnn1_own": lay(gnn1[:D]),
        "w_gnn1_agg": lay(gnn1[D:]),
        "bias_gnn1": lay(np.broadcast_to(np.asarray(L1_gnn_bias), (P, D))),
        "w_experts": lay(np.stack(weights)),
        "b1": lay(np.stack(b1, 1)),
        "b2": lay(np.stack(b2, 1)),
        "w_gate": lay(np.concatenate([np.asarray(L0_ffn_gate_w), np.asarray(L1_ffn_Wg)], 1)),
        "b_gate": lay(np.broadcast_to(gate_b, (P, 2 * E))),
        "ident": np.eye(P, dtype=np.float32),
        "select": np.concatenate([np.eye(E, dtype=np.float32)] * 2),
        "below": lay(np.broadcast_to((e[None, :] < e[:, None]).astype(np.float32).reshape(-1), (P, E * E))),
    }
    nc = bacc.Bacc("TRN2", target_bir_lowering=False, num_devices=1, dynamic_dma_scratch_size=1024)
    program(nc, [(k, v.shape) for k, v in arrays.items()])
    r = run_bass_kernel_spmd(nc, [{"in_" + k: v for k, v in arrays.items()}], core_ids=[0])
    got = r.results[0]["out"]
    return got.transpose(1, 0, 2).reshape(N, D)
```

```python
from contextlib import ExitStack

import numpy as np
import concourse.bass as bass
from concourse import mybir

F32 = mybir.dt.float32
F32R = mybir.dt.float32r
ALU = mybir.AluOpType
ACT = mybir.ActivationFunctionType
AX = mybir.AxisListType

P = 128
N = 8192
D = 128
E = 8
H = 256
TOPK = 2
PW = 1024
NP = N // PW
JB = N // P
TT = PW // P
CH = 512
CT = CH // P
NC = PW // CH
RING = 4
WIDE = 2 * RING
WT = 2 * E * H // PW
UNITS = NC * E
LEAD = 3
LN_EPS = 1e-5
W_AT = 2 * RING
W_IN = (0, NP + 1)
ROW_TILES = NP * TT * 8


def schedule(kind, tiles=JB, lead=0):
    at = {}

    def put(pos, *what):
        at.setdefault(pos, []).append(what)

    def front(s, c, spread=(2, 4, 6, 9, 12, 15, 17, 20, 24)):
        put(s - 1, "own_sum", 1, c)
        for step, what in zip(spread, ("own_turn", "graph_out", "moments", "normalise", "turn", "gate",
                                       "softmax", "choose", "weights_turn")):
            put(s + step, what, 1, c)

    def units(s, spacing, back, c):
        for e in range(E):
            put(s + int(spacing * e), "unit", back, c, e)
            put(s + int(spacing * (e + 1)), "second", back, c, e)

    def next_y(s, p, c):
        for step, what in zip((0, 1, 3, 5, 7) if kind == "finish" else (0, 2, 4, 7, 9),
                              ("next1", "next_root", "next2", "next_hi", "next3")):
            put(s + step, what, p, c)

    if kind in ("second", "steady") and tiles < JB:
        put(JB - 1, "save", 1, 0)
    if kind == "steady" and tiles == JB or kind == "finish" and not tiles:
        put(-1, "save", 2, 0)
    if kind in ("steady", "finish"):
        put(-1 if kind == "finish" else 2 if tiles < JB else 1, "add", 2, 0)
    if kind == "second":
        front(0, 0)
        front(32, 1)
        units(31, 4, 1, 0)
    if kind == "steady":
        front(2, 0)
        units(-1, 4, 2, 1)
        put(32, "save", 2, 1)
        put(35 if tiles < JB else 34, "add", 2, 1)
        if tiles < JB:
            next_y(38, (JB - tiles) // TT - 2, 0)
            next_y(50, (JB - tiles) // TT - 2, 1)
        front(35, 1)
        units(31, 4, 1, 0)
    if kind == "finish":
        front(0, 0, range(2, 20, 2))
        front(10, 1, range(2, 20, 2))
        units(-1, 1.5, 2, 1)
        units(19, 1.5, 1, 0)
        units(31, 1.5, 1, 1)
        for pos, back, c in ((11, 2, 1), (31, 1, 0), (43, 1, 1)):
            put(pos, "save", back, c)
            put(pos + (0 if back == 2 else 1), "add", back, c)
        if tiles:
            for pos, p, c in ((14, NP - 2, 0), (22, NP - 2, 1), (34, NP - 1, 0), (46, NP - 1, 1)):
                next_y(pos, p, c)
    if kind == "first":
        for k, stages in AFTER.items():
            for name, c in stages:
                put(k if k != CLOSE else 4 if name == "sum_cols" else -1, name, 0, c)
    for stages in at.values():
        stages.sort(key=lambda w: ORDER.index(w[0]) if w[0] in ORDER else len(ORDER))
    slots = [-1 - -(JB * (k + 1) // tiles) for k in range(tiles)]
    if not tiles:
        yield ("acc", 1, 0)
    for pos in range(-1, JB + lead):
        for k in range(tiles):
            if slots[k] == pos:
                yield ("tile", JB - tiles + k)
                if k == 0 and kind != "first":
                    yield ("acc", 1, 0)
        if pos < JB - 1:
            yield from at.get(pos - (lead if tiles else 0), ())
        elif pos == JB - 1:
            for late in range(pos - (lead if tiles else 0), JB):
                yield from at.get(late, ())


def ahead(tiles):
    return LEAD * JB // max(tiles, 1) if tiles else 0


ORDER = ("unit", "second", "save", "add")

CLOSE = RING - 1
AFTER = {CLOSE: (("sum_hi", 0), ("sum_lo", 0), ("sum_cols", 0), ("saved", 0)), 6: (("close", 0),),
         8: (("degrees_root", 0),), 9: (("degrees", 0), ("next1", 0)), 10: (("next_root", 0),), 15: (("next2", 0),),
         17: (("next_hi", 0),), 23: (("next3", 0), ("next1", 1)), 24: (("next_root", 1),), 31: (("next2", 1),),
         33: (("next_hi", 1),), 39: (("next3", 1), ("low_out", 0)), 43: (("low_out", 1),), 47: (("low_add", 0),),
         51: (("low_add", 1),)}


def by_pool(jb):
    return jb % 5 % 2 == 0


def row_pass(p):
    rows = [[("row", t, c) for c in range(p, NP)] for t in range(TT)]
    cols = [[("col", jb) for jb in range(t * p, (t + 1) * p)] for t in range(TT)]
    if p == 1:
        return sum(rows, []) + sum(cols, [])
    return sum((r + c for r, c in zip(rows, cols)), [])


def index(G, jb):
    if isinstance(G, int) and G < NP:
        return LOW + sum(JB - q * TT for q in range(G)) + jb - G * TT
    return G * JB + jb


LOW = sum(p * TT for p in range(NP))


class Steps:

    def __init__(self, eng, sem):
        self.eng, self.sem, self.done, self.shift = eng, sem, 0, None

    def loop(self, var, first, per, times):
        self.shift, self.start, self.per, self.times = (var - first) * per, self.done, per, times

    def end_loop(self):
        assert self.done == self.start + self.per, (self.done - self.start, self.per)
        self.done, self.shift = self.start + self.per * self.times, None

    def wait(self, ins):
        ins.then_inc(self.sem, 1)
        self.done += 1
        self.eng.wait_ge(self.sem, self.done if self.shift is None else self.shift + self.done)


def two_layers(nc, x, adj_rows, adj_cols, w_gnn0, w_gnn1_own, w_gnn1_agg, bias_gnn1, w_experts,
               b1, b2, w_gate, b_gate, ident_in, select_in, below_in, out):
    ctx = ExitStack()
    with ctx:
        def sb(name, shape, dt=F32):
            return ctx.enter_context(nc.sbuf_tensor(name, shape, dt))

        def sem(name):
            return ctx.enter_context(nc.semaphore(name))

        xs = sb("xs", [P, JB, D])
        y_hi = sb("y_hi", [P, JB, D], F32R)
        y_lo = sb("y_lo", [P, JB, D], F32R)
        raw = sb("raw", [P, RING, PW])
        a_hi = sb("a_hi", [P, RING, PW], F32R)
        a_lo = sb("a_lo", [P, RING, PW], F32R)
        with nc.sbuf_tensor("early", [P, WIDE - RING, PW], F32) as early:
            pass
        w_hi = sb("w_hi", [P, WT, PW], F32R)
        w_lo = sb("w_lo", [P, WT, PW], F32R)
        xn = sb("xn", [P, TT, D])
        xt_hi = sb("xt_hi", [P, NC, CH], F32R)
        xt_lo = sb("xt_lo", [P, NC, CH], F32R)
        act = sb("act", [P, 2, CH])
        g_hi = sb("g_hi", [P, 2, CH], F32R)
        g_lo = sb("g_lo", [P, 2, CH], F32R)
        acc_s = sb("acc_s", [P, NC, CH])
        cmp_gt = sb("cmp_gt", [P, CT, E, E])
        cmp_eq = sb("cmp_eq", [P, CT, E, E])
        turn = sb("turn", [P, CT, D])
        cw_t = sb("cw_t", [2 * E, NC, CH], F32R)
        wg0 = sb("wg0", [P, D])
        wg1_agg = sb("wg1_agg", [P, D])
        wg1_own_hi = sb("wg1_own_hi", [P, D], F32R)
        wg1_own_lo = sb("wg1_own_lo", [P, D], F32R)
        bias1 = sb("bias1", [P, D])
        ident = sb("ident", [P, P])
        gate = sb("gate", [P, 2 * E])
        gate_hi = sb("gate_hi", [P, 2 * E], F32R)
        gate_lo = sb("gate_lo", [P, 2 * E], F32R)
        gate_b = sb("gate_b", [P, 2 * E])
        eb1 = sb("eb1", [P, 2, 2 * E])
        eb2_hi = sb("eb2_hi", [2 * E, 2, D], F32R)
        eb2_lo = sb("eb2_lo", [2 * E, 2, D], F32R)
        ones = sb("ones", [P, 1], F32R)
        select = sb("select", [2 * E, E])
        select_r = sb("select_r", [2 * E, E], F32R)
        below = sb("below", [P, E * E])
        sums = sb("sums", [P, 2, TT, 8])
        d_is = sb("d_is", [P, JB])
        deg = sb("deg", [P, TT])
        stats = sb("stats", [P, CT, 6])
        mv = sb("mv", [P, CT, 2])
        rstd = sb("rstd", [P, CT])
        n_stats = sb("n_stats", [P, CT, 6])
        n_mv = sb("n_mv", [P, CT, 2])
        n_rstd = sb("n_rstd", [P, CT])
        pad = sb("pad", [P, 1])
        minus_half = sb("minus_half", [P, TT])
        lg = sb("lg", [P, CT, E])
        pr = sb("pr", [P, CT, E])
        top = sb("top", [P, CT])
        inv = sb("inv", [P, CT])
        rank = sb("rank", [P, CT, E])
        cw = sb("cw", [P, CT, E])
        cw_pair = sb("cw_pair", [P, CT, 2 * E], F32R)
        wg1_own = act[:, 0, 0:D]
        eb2 = act[0:2 * E, 1, 0:2 * D].rearrange("p (l d) -> p l d", l=2)

        acc = ctx.enter_context(nc.psum_tensor("acc", [P, NC, CH], F32))
        hid = ctx.enter_context(nc.psum_tensor("hid", [P, 2, CH], F32))
        cwb = ctx.enter_context(nc.psum_tensor("cwb", [P, CH], F32))
        yps = ctx.enter_context(nc.psum_tensor("yps", [P, CH], F32))
        mix = ctx.enter_context(nc.psum_tensor("mix", [P, NC, CH], F32))

        consts_in = sem("consts_in")
        x_in = sem("x_in")
        landed = [sem(f"landed{i}") for i in range(WIDE)]
        consts_hi = sem("consts_hi")
        consts_lo = sem("consts_lo")
        row_sum_act = sem("row_sum_act")
        row_sum_dve = sem("row_sum_dve")
        col_added = sem("col_added")
        col_cleared = sem("col_cleared")
        sum_hi_made = sem("sum_hi_made")
        sum_lo_made = sem("sum_lo_made")
        col_sums_psum = sem("col_sums_psum")
        w_hi_made = sem("w_hi_made")
        w_lo_made = sem("w_lo_made")
        a_hi_made = sem("a_hi_made")
        a_lo_made = sem("a_lo_made")
        a_used = sem("a_used")
        y_made = sem("y_made")
        y_hi_made = sem("y_hi_made")
        y_lo_made = sem("y_lo_made")
        acc_saved = sem("acc_saved")
        xn_made = sem("xn_made")
        xt_psum = sem("xt_psum")
        xt_hi_made = sem("xt_hi_made")
        xt_lo_made = sem("xt_lo_made")
        graph_psum = sem("graph_psum")
        low_added = sem("low_added")
        gate_psum = sem("gate_psum")
        logits_made = sem("logits_made")
        exp_made = sem("exp_made")
        cw_made = sem("cw_made")
        cwt_psum = sem("cwt_psum")
        cwt_made = sem("cwt_made")
        cwb_psum = sem("cwb_psum")
        hid_psum = sem("hid_psum")
        gelu_made = sem("gelu_made")
        scaled = sem("scaled")
        g_hi_made = sem("g_hi_made")
        g_lo_made = [sem(f"g_lo_made{i}") for i in range(2)]
        y_done = sem("y_done")
        y_saved = sem("y_saved")
        out_psum = sem("out_psum")
        out_added = sem("out_added")
        compared = sem("compared")
        rank_made = sem("rank_made")
        pool_step = sem("pool_step")
        dve_step = sem("dve_step")
        half_set = sem("half_set")
        deg_made = sem("deg_made")
        deg_rooted = sem("deg_rooted")
        next_var = sem("next_var")
        next_rstd = sem("next_rstd")
        token_var = sem("token_var")
        token_rstd = sem("token_rstd")
        stored = sem("stored")

        consts = [(wg0, w_gnn0), (wg1_agg, w_gnn1_agg), (wg1_own, w_gnn1_own), (bias1, bias_gnn1),
                  (ident, ident_in), (gate, w_gate), (gate_b, b_gate), (eb1, b1), (eb2, b2),
                  (select, select_in), (below, below_in)]
        splits = [(wg1_own, wg1_own_hi, wg1_own_lo), (gate, gate_hi, gate_lo), (eb2, eb2_hi, eb2_lo)]

        LATER = NP - 1

        def turns(G, layer, again, c):
            return G * NC + c if layer == 0 else NC * NP + (G - NP) * 2 * NC + 2 * c + again

        def tile_use(G, jb):
            before = ROW_TILES * RING // WIDE - LOW
            if not isinstance(G, int) or (G, jb) >= (W_IN[0], W_AT):
                before += WT
            if not isinstance(G, int) or (G, jb) >= (W_IN[1], W_AT):
                before += WT
            return (before + index(G, jb)) // RING if isinstance(G, int) \
                else G * (JB // RING) + (before + jb) // RING

        def panel(t, G, layer, n=TT, first=0):
            if isinstance(G, int):
                a = (G - layer * NP) * TT + first
                return t[:, a:a + n]
            return t[:, bass.ds((G - layer * NP) * TT + first, n)]

        passes = [row_pass(p) for p in range(NP)]
        summed = {}
        for p in range(NP):
            for what, *n in passes[p]:
                if what == "row":
                    k = len(summed)
                    summed[(p, *n)] = (k % 2 == 0, k // 2 + 1)

        pooled = {}
        for p in range(NP):
            for jb in range(p * TT):
                if by_pool(jb):
                    pooled[p, jb] = len(pooled) + 1
        added = xn[:].rearrange("p t d -> p (t d)")

        def col_sums(p, c):
            return hid[:, c] if p % 2 == 0 else (cwb, yps)[c][:]

        def cw_bank(e, tail):
            return acc[:, 0] if tail and e % 2 else cwb[:]

        def halves(e, tail):
            if tail and e % 2:
                return [t[:, 0].rearrange("p (h n) -> p h n", h=2) for t in (raw, a_hi, a_lo)]
            return act[:], g_hi[:], g_lo[:]

        def lag(e, tail):
            return 1 if tail and e > 0 else 0

        def pooled_by(p):
            return max(n for (q, _), n in pooled.items() if q <= p)

        def wait_freed(eng, p, item):
            what, *n = item
            if what == "col":
                eng.wait_ge(a_lo_made, index_low(p, n[0]) + 1)
                if by_pool(n[0]):
                    eng.wait_ge(col_added, pooled[p, n[0]])
            else:
                by_act, count = summed[(p, *n)]
                eng.wait_ge(row_sum_act if by_act else row_sum_dve, count)

        def wide(k):
            s = k % WIDE
            return raw[:, s] if s < RING else early[:, s - RING]

        def index_low(p, jb):
            return sum(q * TT for q in range(p)) + jb

        block = ctx.enter_context(nc.Block())

        @block.sync
        def _(sp):
            sp.dma_start(xs[:], x).then_inc(x_in, 16)
            for t, src in consts:
                sp.dma_start(t[:], src).then_inc(consts_in, 16)

            for p in range(NP):
                for k, (what, *n) in enumerate(passes[p]):
                    if p or k >= WIDE:
                        before = (p, passes[p][k - WIDE]) if k >= WIDE else (p - 1, passes[p - 1][k - WIDE])
                        wait_freed(sp, *before)
                    src = adj_rows[p * TT + n[0], n[1]] if what == "row" else adj_cols[p, n[0]]
                    sp.dma_start(wide(k), src).then_inc(landed[k % WIDE], 16)

            def weight_tiles(layer):
                for i in range(WT):
                    sp.wait_ge(a_lo_made, index(W_IN[layer], W_AT + i) - RING + 1)
                    sp.dma_start(raw[:, i], w_experts[layer, i]).then_inc(landed[i], 16)

            def col_tiles(G, layer):
                for jb in range((G * TT if layer == 0 else 0), JB):
                    if isinstance(G, int) and (G, jb) == (W_IN[layer], W_AT):
                        weight_tiles(layer)
                    if isinstance(G, int) and (G, jb) < (0, RING):
                        wait_freed(sp, NP - 1, passes[NP - 1][jb - WIDE])
                    elif isinstance(G, int) and G in W_IN and W_AT <= jb < W_AT + WT:
                        sp.wait_ge(w_lo_made, layer * WT + jb - W_AT + 1)
                    else:
                        sp.wait_ge(a_lo_made, index(G, jb) - RING + 1)
                    src = adj_cols[G - layer * NP, jb] if isinstance(G, int) else \
                        adj_cols[bass.ds(G - layer * NP, 1), jb].rearrange("o p n -> (o p) n")
                    sp.dma_start(raw[:, jb % RING], src).then_inc(landed[jb % RING], 16)

            for G in range(NP):
                col_tiles(G, 0)
            col_tiles(NP, 1)
            col_tiles(NP + 1, 1)
            with sp.Fori(NP + 2, 2 * NP) as G:
                col_tiles(G, 1)
            for p in range(NP):
                for c in range(NC):
                    sp.wait_ge(out_added, (NP + p) * NC + c + 1)
                    a = p * TT + c * CT
                    sp.dma_start(out[:, a:a + CT], xs[:, a:a + CT]).then_inc(stored, 16)
            sp.wait_ge(stored, 16 * NP * NC)

        @block.tensor
        def _(pe):
            def three(o, l_hi, l_lo, r_hi, r_lo, start, stop):
                pe.matmul(o, l_hi, r_hi, start=start, stop=False)
                pe.matmul(o, l_hi, r_lo, start=False, stop=False)
                return pe.matmul(o, l_lo, r_hi, start=False, stop=stop)

            def product(jb, first, last):
                s = jb % RING
                for hi_or_lo, left in ((a_hi, y_hi), (a_lo, y_hi), (a_hi, y_lo)):
                    for c in range(NC):
                        mm = pe.matmul(acc[:, c], left[:, jb], hi_or_lo[:, s, c * CH:(c + 1) * CH],
                                       start=(first and hi_or_lo is a_hi and left is y_hi),
                                       stop=(last and left is y_lo))
                mm.then_inc(a_used, 1)

            def low_tile(p, jb):
                if jb == 0 and p > 1:
                    pe.wait_ge(acc_saved, p - 1)
                    pe.wait_ge(deg_made, p - 1)
                if jb % CT == 0:
                    pe.wait_ge(y_lo_made, jb // CT + 1)
                pe.wait_ge(a_lo_made, index_low(p, jb) + 1)
                for part in () if by_pool(jb) else (a_hi, a_lo):
                    for c in range(NC):
                        pe.matmul(col_sums(p, c), ones[:].broadcast_to([P, P]), part[:, jb % RING, c * CH:(c + 1) * CH],
                                  start=(jb == 1 and part is a_hi), stop=False)
                product(jb, jb == 0, jb == p * TT - 1)

            def sum_cols(p):
                pe.wait_ge(sum_lo_made, p)
                for part in (xt_hi, xt_lo):
                    for c in range(NC):
                        mm = pe.matmul(col_sums(p, c), ones[:].broadcast_to([P, P]), part[:, c],
                                       start=False, stop=(part is xt_lo))
                mm.then_inc(col_sums_psum, 1)

            def tile(G, layer, jb, first_panel):
                first = jb == (G * TT if layer == 0 else 0)
                if first:
                    pe.wait_ge(acc_saved, G + LATER)
                if first_panel and jb % CT == 0:
                    pe.wait_ge(y_lo_made, layer * NP * NC + jb // CT + 1)
                pe.wait_ge(a_lo_made, index(G, jb) + 1)
                product(jb, first, jb == JB - 1)

            def low_out(n, c):
                pe.wait_ge(acc_saved, n + 1)
                if n > 0:
                    pe.wait_ge(low_added, (n - 1) * NC + c + 1)
                for t in range(CT):
                    mm = pe.matmul(mix[:, c, t * P:(t + 1) * P], acc_s[:, c, t * P:(t + 1) * P], wg0[:],
                                   start=True, stop=True)
                mm.then_inc(graph_psum, 1)

            def bank_free(G, c):
                if isinstance(G, int) and G == 0:
                    pe.wait_ge(low_added, (LATER - 1) * NC + c + 1)
                else:
                    pe.wait_ge(out_added, (G - 1) * NC + c + 1)

            def turn_chunk(G, layer, again, c):
                if layer == 1 and not again:
                    bank_free(G, c)
                pe.wait_ge(xn_made, turns(G, layer, again, c) + 1)
                for t in range(CT):
                    mm = pe.transpose(mix[:, c, t * P:(t + 1) * P], xn[:, c * CT + t], ident[:])
                mm.then_inc(xt_psum, 1)

            def graph_out(G, layer, c):
                pe.wait_ge(acc_saved, G + 1 + LATER)
                if layer == 0:
                    bank_free(G, c)
                if layer == 1:
                    pe.wait_ge(xt_lo_made, turns(G, 1, 0, c) + 1)
                for t in range(CT):
                    o = mix[:, c, t * P:(t + 1) * P]
                    col = slice(t * P, (t + 1) * P)
                    if layer == 1:
                        pe.matmul(o, xt_hi[:, c, col], wg1_own_hi[:], start=True, stop=False)
                        pe.matmul(o, xt_hi[:, c, col], wg1_own_lo[:], start=False, stop=False)
                        pe.matmul(o, xt_lo[:, c, col], wg1_own_hi[:], start=False, stop=False)
                    mm = pe.matmul(o, acc_s[:, c, col], (wg1_agg if layer else wg0)[:],
                                   start=(layer == 0), stop=True)
                mm.then_inc(graph_psum, 1)

            def gates(G, layer, c):
                pe.wait_ge(xt_lo_made, turns(G, layer, layer, c) + 1)
                ge = slice(layer * E, (layer + 1) * E)
                for t in range(CT):
                    col = slice(t * P, (t + 1) * P)
                    mm = three(mix[:, c, t * E:(t + 1) * E], xt_hi[:, c, col], xt_lo[:, c, col],
                               gate_hi[:, ge], gate_lo[:, ge], True, True)
                mm.then_inc(gate_psum, 1)

            def weights_turn(G, c):
                pe.wait_ge(cw_made, G * NC + c + 1)
                for t in range(CT):
                    mm = pe.transpose(mix[0:2 * E, c, t * P:(t + 1) * P], cw_pair[:, t].bitcast(F32), ident[:])
                mm.then_inc(cwt_psum, 1)

            def unit(G, layer, c, e, tail):
                u = G * UNITS + c * E + e
                bank = cw_bank(e, tail)
                if isinstance(G, int) and G == layer * NP and c + e == 0:
                    pe.wait_ge(w_lo_made, (layer + 1) * WT)
                for half in range(2):
                    if not (isinstance(G, int) and G == 0 and c + e == 0):
                        pe.wait_ge(gelu_made, (u - 1) * 2 + half + 1)
                    col = e * H + half * P
                    three(hid[:, half], w_hi[:, col // PW, col % PW:col % PW + P],
                          w_lo[:, col // PW, col % PW:col % PW + P], xt_hi[:, c], xt_lo[:, c],
                          True, True).then_inc(hid_psum, 1)
                if not (isinstance(G, int) and G == 0 and c + e == 0):
                    pe.wait_ge(scaled, u * 2 - (2 if tail else 0))
                if e == 0:
                    pe.wait_ge(cwt_made, G * NC + c + 1)
                if tail and e == 1:
                    pe.wait_ge(acc_saved, 2 * NP + LATER)
                pe.matmul(bank, select_r[:, e:e + 1].broadcast_to([2 * E, P]), cw_t[:, c],
                          start=True, stop=True).then_inc(cwb_psum, 1)

            def second(G, layer, c, e, tail):
                _, hi, lo = halves(e, tail)
                if e == 0:
                    if not (isinstance(G, int) and G == 0 and c == 0):
                        pe.wait_ge(y_saved, G * NC + c)
                    pe.matmul(yps[:], eb2_hi[:, layer], cw_t[:, c], start=True, stop=False)
                    pe.matmul(yps[:], eb2_lo[:, layer], cw_t[:, c], start=False, stop=False)
                for half in range(2):
                    v = (G * UNITS + c * E + e) * 2 + half
                    col = (e * 2 + half) * D
                    l_hi = w_hi[:, WT // 2 + col // PW, col % PW:col % PW + D]
                    l_lo = w_lo[:, WT // 2 + col // PW, col % PW:col % PW + D]
                    pe.wait_ge(g_hi_made, v + 1)
                    pe.matmul(yps[:], l_hi, hi[:, half], start=False, stop=False)
                    pe.matmul(yps[:], l_lo, hi[:, half], start=False, stop=False)
                    pe.wait_ge(g_lo_made[half], G * UNITS + c * E + e + 1)
                    pe.matmul(yps[:], l_hi, lo[:, half], start=False,
                              stop=(e == E - 1 and half == 1)).then_inc(y_done, 1)

            def add(G, c):
                pe.wait_ge(y_saved, G * NC + c + 1)
                for t in range(CT):
                    mm = pe.transpose(mix[:, c, t * P:(t + 1) * P], turn[:, t], ident[:])
                mm.then_inc(out_psum, 1)

            def run(G, kind, layer, e_layer, tiles=JB, first_panel=False):
                for what, *n in schedule(kind, tiles):
                    if what == "tile":
                        tile(G, layer, n[0], first_panel)
                        continue
                    back, c, *e = n
                    if what == "sum_cols":
                        sum_cols(NP - 1)
                    elif what == "low_out":
                        low_out(LATER - 1, c)
                    elif what == "own_turn" and e_layer == 1:
                        turn_chunk(G - back, 1, 0, c)
                    elif what == "graph_out":
                        graph_out(G - back, e_layer, c)
                    elif what == "turn":
                        turn_chunk(G - back, e_layer, e_layer, c)
                    elif what == "gate":
                        gates(G - back, e_layer, c)
                    elif what == "weights_turn":
                        weights_turn(G - back, c)
                    elif what == "unit":
                        unit(G - back, e_layer, c, *e, not tiles)
                    elif what == "second":
                        second(G - back, e_layer, c, *e, not tiles)
                    elif what == "add":
                        add(G - back, c)

            pe.wait_ge(consts_lo, 1)
            for p in range(NP):
                for k, (what, *n) in enumerate(passes[p]):
                    if what == "col":
                        low_tile(p, n[0])
                    for stage, c in AFTER.get(k, ()) if p > 1 else ():
                        if stage == "sum_cols":
                            sum_cols(p - 1)
                        elif stage == "low_out":
                            low_out(p - 2, c)
            run(0, "first", 0, 0, first_panel=True)
            run(1, "second", 0, 0, JB - TT)
            for G in range(2, NP):
                run(G, "steady", 0, 0, JB - G * TT)
            run(NP, "finish", 1, 0, first_panel=True)
            run(NP + 1, "second", 1, 1)
            with pe.Fori(NP + 2, 2 * NP) as G:
                run(G, "steady", 1, 1)
            run(2 * NP, "finish", 1, 1, tiles=0)

        @block.scalar
        def _(sc):
            def copy(o, i):
                return nc.scalar.activation(o, i, ACT.Copy)

            sc.wait_ge(consts_in, 16 * len(consts))
            copy(select_r[:], select[:])
            for full, hi, _ in splits:
                ins = copy(hi[:], full[:])
            ins.then_inc(consts_hi, 1)

            def next_y(count, p, layer, half):
                sc.wait_ge(y_made, count + 1)
                if layer == 1:
                    sc.wait_ge(a_used, index(p - NP, (p - NP + 1) * TT - 1) + 1)
                copy(panel(y_hi, p, layer, CT, half * CT), turn[:]).then_inc(y_hi_made, 1)

            def save_low(n):
                sc.wait_ge(a_used, sum(q * TT for q in range(n + 2)))
                if n > 0:
                    sc.wait_ge(graph_psum, n * NC)
                copy(acc_s[:], acc[:]).then_inc(acc_saved, 1)

            def sum_hi(p):
                sc.wait_ge(col_added, pooled_by(p))
                copy(xt_hi[:].rearrange("p c n -> p (c n)"), added).then_inc(sum_hi_made, 1)

            def high(full, s, use, at, used):
                sc.wait_ge(landed[s], (use + 1) * 16)
                if used is not None:
                    sc.wait_ge(a_used, used)
                copy(a_hi[:, at], full).then_inc(a_hi_made, 1)

            for p in range(NP):
                for k, (what, *n) in enumerate(passes[p]):
                    s, use = k % WIDE, (p * JB + k) // WIDE
                    if what == "col":
                        i = index_low(p, n[0])
                        high(wide(k), s, use, i % RING, i - RING + 1 if i >= RING else None)
                    elif summed[(p, *n)][0]:
                        if n[0] == 0 and p > 1:
                            sc.wait_ge(deg_made, p - 1)
                        sc.wait_ge(landed[s], (use + 1) * 16)
                        nc.scalar.activation(wide(k), wide(k), ACT.Copy,
                                             accum_out=sums[:, p % 2, n[0], n[1]:n[1] + 1]).then_inc(row_sum_act, 1)
                    for stage, half in AFTER.get(k, ()):
                        if stage == "sum_hi" and p > 1:
                            sum_hi(p - 1)
                        elif stage == "saved" and p > 1:
                            save_low(p - 2)
                        elif stage == "next_hi" and p > 0:
                            next_y((p - 1) * NC + half, p - 1, 0, half)

            def weights(layer):
                for i in range(WT):
                    n = tile_use(W_IN[layer], W_AT) - 1
                    if layer == 0 and i == 0:
                        sc.wait_ge(a_lo_made, LOW)
                        sc.wait_ge(row_sum_dve, len(summed) // 2)
                        sc.wait_ge(col_added, len(pooled))
                    sc.wait_ge(landed[i], (n + 1) * 16)
                    copy(w_hi[:, i], raw[:, i]).then_inc(w_hi_made, 1)

            def tile(G, jb):
                if isinstance(G, int) and G in W_IN and jb == W_AT:
                    weights(W_IN.index(G))
                high(raw[:, jb % RING], jb % RING, tile_use(G, jb), jb % RING, index(G, jb) - RING + 1)

            def turned(G, layer, again, c):
                sc.wait_ge(xt_psum, turns(G, layer, again, c) + 1)
                copy(xt_hi[:, c], mix[:, c]).then_inc(xt_hi_made, 1)

            def unit(G, layer, c, e, tail):
                hidden, hi, _ = halves(e, tail)
                start = isinstance(G, int) and G == 0 and c + e == 0
                for half in range(2):
                    v = (G * UNITS + c * E + e) * 2 + half
                    sc.wait_ge(hid_psum, v + 1)
                    if not start:
                        sc.wait_ge(g_lo_made[half], G * UNITS + c * E + e - lag(e, tail))
                    b = (layer, e * 2 + half)
                    nc.scalar.activation(hidden[:, half], hid[:, half], ACT.Gelu,
                                         bias=eb1[:, b[0], b[1]:b[1] + 1]).then_inc(gelu_made, 1)
                for half in range(2):
                    v = (G * UNITS + c * E + e) * 2 + half
                    sc.wait_ge(scaled, v + 1)
                    if not start:
                        sc.wait_ge(y_done, v - 1 - 2 * lag(e, tail))
                    copy(hi[:, half], hidden[:, half]).then_inc(g_hi_made, 1)

            nexts = NP * NC

            def save(G, c, last):
                sc.wait_ge(y_done, (G * UNITS + (c + 1) * E) * 2)
                if last is not None:
                    sc.wait_ge(y_lo_made, last)
                if not (isinstance(G, int) and G == 0 and c == 0):
                    sc.wait_ge(out_psum, G * NC + c)
                copy(turn[:].rearrange("p t d -> p (t d)"), yps[:]).then_inc(y_saved, 1)

            def run(G, kind, layer, e_layer, tiles=JB):
                nonlocal nexts
                for what, *n in schedule(kind, tiles, ahead(tiles)):
                    if what == "tile":
                        tile(G, n[0])
                        continue
                    back, c, *e = n
                    if what == "acc":
                        sc.wait_ge(a_used, index(G - 1, JB - 1) + 1)
                        if isinstance(G, int) and G == 1:
                            sc.wait_ge(graph_psum, LATER * NC)
                        copy(acc_s[:], acc[:]).then_inc(acc_saved, 1)
                    elif what == "own_turn" and e_layer == 1:
                        turned(G - back, 1, 0, c)
                    elif what == "turn":
                        turned(G - back, e_layer, e_layer, c)
                    elif what == "gate" and e_layer == 0:
                        q = (G - back) * NC + c
                        sc.wait_ge(logits_made, q + 1)
                        nc.scalar.activation(pr[:], lg[:], ACT.Exp).then_inc(exp_made, 1)
                    elif what == "weights_turn":
                        q = (G - back) * NC + c
                        sc.wait_ge(cwt_psum, q + 1)
                        copy(cw_t[:, c], mix[0:2 * E, c]).then_inc(cwt_made, 1)
                    elif what == "unit":
                        unit(G - back, e_layer, c, *e, not tiles)
                    elif what == "save":
                        save(G - back, c, nexts if e_layer == 0 else None)
                    elif what == "next_hi" and kind != "first":
                        next_y(nexts, NP + back, 1, c)
                        nexts += 1
                    elif what == "next_hi":
                        next_y((NP - 1) * NC + c, NP - 1, 0, c)
                    elif what == "sum_hi":
                        sum_hi(NP - 1)
                    elif what == "saved":
                        save_low(LATER - 1)

            run(0, "first", 0, 0)
            run(1, "second", 0, 0, JB - TT)
            for G in range(2, NP):
                run(G, "steady", 0, 0, JB - G * TT)
            run(NP, "finish", 1, 0)
            run(NP + 1, "second", 1, 1)
            with sc.Fori(NP + 2, 2 * NP) as G:
                run(G, "steady", 1, 1)
            run(2 * NP, "finish", 1, 1, tiles=0)

        @block.gpsimd
        def _(pool):
            def root(t, n, made, done, count):
                pool.wait_ge(made, count + 1)
                nc.gpsimd.tensor_tensor(t[:, 0:n], t[:, 0:n], minus_half[:, 0:n], ALU.pow).then_inc(done, 1)

            def after(stage, p, half):
                if stage == "degrees_root":
                    root(deg, TT, deg_made, deg_rooted, p)
                elif stage == "next_root":
                    root(n_rstd, CT, next_var, next_rstd, p * NC + half)

            def add_col(p, k, jb):
                if jb == 0:
                    if p > 1:
                        pool.wait_ge(sum_lo_made, p - 1)
                    nc.gpsimd.memset(added, 0.0).then_inc(col_cleared, 1)
                    pool.wait_ge(col_cleared, p)
                else:
                    pool.wait_ge(col_added, pooled[p, jb] - 1)
                pool.wait_ge(landed[k % WIDE], ((p * JB + k) // WIDE + 1) * 16)
                nc.gpsimd.tensor_tensor(added, added, wide(k), ALU.add).then_inc(col_added, 1)

            def rank_of(q):
                pool.wait_ge(compared, q + 1)
                eq = cmp_eq[:].rearrange("p t a b -> p t (a b)")
                nc.gpsimd.tensor_tensor(eq, eq, below[:].unsqueeze(1).broadcast_to([P, CT, E * E]),
                                        ALU.mult).then_inc(pool_step, 1)
                pool.wait_ge(pool_step, q + 1)
                nc.gpsimd.tensor_tensor(cmp_gt[:], cmp_gt[:], cmp_eq[:], ALU.add).then_inc(rank_made, 1)

            def unit(G, c, e, tail):
                hidden, hi, lo = halves(e, tail)
                for half in range(2):
                    pool.wait_ge(g_hi_made, (G * UNITS + c * E + e) * 2 + half + 1)
                    nc.gpsimd.tensor_tensor(lo[:, half], hidden[:, half], hi[:, half].bitcast(F32),
                                            ALU.subtract).then_inc(g_lo_made[half], 1)

            def next_low(i):
                pool.wait_ge(y_hi_made, NP * NC + i + 1)
                y = slice(i * CT, (i + 1) * CT)
                nc.gpsimd.tensor_tensor(y_lo[:, y], turn[:], y_hi[:, y].bitcast(F32),
                                        ALU.subtract).then_inc(y_lo_made, 1)

            def run(G, kind, tiles=JB):
                for what, *n in schedule(kind, tiles, ahead(tiles)):
                    if what == "tile":
                        continue
                    back, c, *e = n
                    if what == "moments":
                        root(rstd, CT, token_var, token_rstd, (G - back) * NC + c)
                    elif what == "softmax":
                        rank_of((G - back) * NC + c)
                    elif what == "unit":
                        unit(G - back, c, *e, not tiles)
                    elif what == "next3":
                        next_low(back * NC + c)
                    elif what == "next_root":
                        root(n_rstd, CT, next_var, next_rstd, NP * NC + back * NC + c)

            nc.gpsimd.memset(minus_half[:], -0.5).then_inc(half_set, 1)
            pool.wait_ge(half_set, 1)
            for p in range(NP):
                for k, (what, *n) in enumerate(passes[p]):
                    if what == "col" and by_pool(n[0]):
                        add_col(p, k, n[0])
                    for stage, half in AFTER.get(k, ()) if p > 0 else ():
                        after(stage, p - 1, half)
            for k in sorted(AFTER):
                for stage, half in AFTER[k]:
                    after(stage, NP - 1, half)
            run(1, "second", JB - TT)
            for G in range(2, NP):
                run(G, "steady", JB - G * TT)
            run(NP, "finish")
            run(NP + 1, "second")
            with pool.Fori(NP + 2, 2 * NP) as G:
                run(G, "steady")
            run(2 * NP, "finish", tiles=0)

        @block.vector
        def _(ve):
            v = nc.vector
            steps = Steps(ve, dve_step)

            steps.wait(v.memset(ones[:].bitcast(F32), 1.0))
            ve.wait_ge(consts_hi, 1)
            for full, hi, lo in splits:
                ins = v.tensor_tensor(lo[:], full[:], hi[:].bitcast(F32), ALU.subtract)
            ins.then_inc(consts_lo, 1)
            ve.wait_ge(x_in, 16)

            def moments(p, layer, first, n, st, m, r, var_sem):
                v.memset(pad[:], 0.0)
                for t in range(n):
                    ins = v.bn_stats(st[:, t], panel(xs, p, layer, 1, first + t).rearrange("p o d -> p (o d)"))
                steps.wait(ins)
                v.memset(pad[:], 0.0)
                for t in range(n):
                    ins = v.bn_aggr(m[:, t], st[:, t])
                steps.wait(ins)
                v.tensor_scalar(r[:, 0:n], m[:, 0:n, 1], LN_EPS, None, ALU.add).then_inc(var_sem, 1)

            def next1(p, layer, half):
                moments(p, layer, half * CT, CT, n_stats, n_mv, n_rstd, next_var)

            def next2(count, p, layer, half, scale):
                ve.wait_ge(next_rstd, count + 1)
                if count > 0:
                    ve.wait_ge(y_lo_made, count)
                if scale:
                    steps.wait(v.tensor_tensor(n_rstd[:], n_rstd[:],
                                               (d_is[:, half * CT + p * TT:half * CT + p * TT + CT] if isinstance(p, int)
                                                else d_is[:, bass.ds(p * TT + half * CT, CT)]), ALU.mult))
                for t in range(CT):
                    ins = v.tensor_scalar(turn[:, t], panel(xs, p, layer, 1, half * CT + t).rearrange("p o d -> p (o d)"),
                                          n_mv[:, t, 0:1], n_rstd[:, t:t + 1], ALU.subtract, ALU.mult)
                ins.then_inc(y_made, 1)

            def next3(count, p, layer, half):
                ve.wait_ge(y_hi_made, count + 1)
                v.tensor_tensor(panel(y_lo, p, layer, CT, half * CT), turn[:],
                                panel(y_hi, p, layer, CT, half * CT).bitcast(F32),
                                ALU.subtract).then_inc(y_lo_made, 1)

            def degrees(p):
                ve.wait_ge(deg_rooted, p + 1)
                scale = d_is[:, p * TT:(p + 1) * TT] if isinstance(p, int) else d_is[:, bass.ds(p * TT, TT)]
                steps.wait(v.tensor_copy(scale, deg[:]))

            def low(full, at, i):
                ve.wait_ge(a_hi_made, i + 1)
                v.tensor_tensor(a_lo[:, at], full, a_hi[:, at].bitcast(F32),
                                ALU.subtract).then_inc(a_lo_made, 1)

            def close(p):
                for mine, done in ((True, row_sum_act), (False, row_sum_dve)):
                    ve.wait_ge(done, max(n for q, (by_act, n) in summed.items() if by_act == mine and q[0] <= p))
                if p > 0:
                    ve.wait_ge(col_sums_psum, p)
                    diag = act[:].rearrange("p c (t n) -> p (c t) n", n=P)
                    for c in range(NC):
                        ins = v.tensor_tensor(diag[:, c * CT:(c + 1) * CT],
                                              col_sums(p, c).rearrange("p (t n) -> p t n", n=P),
                                              ident[:].unsqueeze(1).broadcast_to([P, CT, P]), ALU.mult)
                    steps.wait(ins)
                    steps.wait(v.tensor_reduce(sums[:, p % 2, :, p - 1], diag, AX.X, ALU.add))
                v.tensor_reduce(deg[:], sums[:, p % 2, :, max(p - 1, 0):], AX.X, ALU.add).then_inc(deg_made, 1)

            def low_out(p, c):
                add_rows(p, c, (p - 1) * NC + c)
                ins = v.memset(pad[:], 0.0)
                ins.then_inc(low_added, 1)

            def add_rows(G, c, count):
                ve.wait_ge(graph_psum, count + 1)
                for t in range(CT):
                    xt = xs[:, G * TT + c * CT + t]
                    col = G * TT + c * CT + t
                    ins = v.scalar_tensor_tensor(xt, mix[:, c, t * P:(t + 1) * P], d_is[:, col:col + 1], xt,
                                                 ALU.mult, ALU.add)
                steps.wait(ins)

            def after(stage, p, half):
                if stage == "degrees":
                    degrees(p)
                elif stage == "next1":
                    next1(p, 0, half)
                elif stage == "next2":
                    next2(p * NC + half, p, 0, half, True)
                elif stage == "next3":
                    next3(p * NC + half, p, 0, half)
                elif stage == "sum_lo" and p > 0:
                    ve.wait_ge(sum_hi_made, p)
                    v.tensor_tensor(xt_lo[:].rearrange("p c n -> p (c n)"), added,
                                    xt_hi[:].rearrange("p c n -> p (c n)").bitcast(F32),
                                    ALU.subtract).then_inc(sum_lo_made, 1)
                elif stage == "close":
                    close(p)
                elif stage == "low_add" and p > 0:
                    low_out(p, half)

            for p in range(NP):
                for k, (what, *n) in enumerate(passes[p]):
                    s, use = k % WIDE, (p * JB + k) // WIDE
                    if what == "col":
                        low(wide(k), n[0] % RING, index_low(p, n[0]))
                    elif not summed[(p, *n)][0]:
                        ve.wait_ge(landed[s], (use + 1) * 16)
                        v.tensor_reduce(sums[:, p % 2, n[0], n[1]:n[1] + 1], wide(k), AX.X,
                                        ALU.add).then_inc(row_sum_dve, 1)
                    for stage, half in AFTER.get(k, ()) if p > 0 else ():
                        after(stage, p - 1, half)

            def weights(layer):
                for i in range(WT):
                    ve.wait_ge(w_hi_made, layer * WT + i + 1)
                    v.tensor_tensor(w_lo[:, i], raw[:, i], w_hi[:, i].bitcast(F32),
                                    ALU.subtract).then_inc(w_lo_made, 1)

            def tile(G, jb):
                if isinstance(G, int) and G in W_IN and jb == W_AT:
                    weights(W_IN.index(G))
                low(raw[:, jb % RING], jb % RING, index(G, jb))

            def turned(G, layer, again, c):
                ve.wait_ge(xt_hi_made, turns(G, layer, again, c) + 1)
                v.tensor_tensor(xt_lo[:, c], mix[:, c], xt_hi[:, c].bitcast(F32),
                                ALU.subtract).then_inc(xt_lo_made, 1)

            def own_sum(G, c):
                v.tensor_tensor(xn[:, c * CT:(c + 1) * CT], panel(y_hi, G, 1, CT, c * CT).bitcast(F32),
                                panel(y_lo, G, 1, CT, c * CT).bitcast(F32), ALU.add).then_inc(xn_made, 1)

            def graph_out(G, layer, c):
                if layer == 0:
                    add_rows(G, c, (LATER + G) * NC + c)
                    return
                ve.wait_ge(graph_psum, (LATER + G) * NC + c + 1)
                for t in range(CT):
                    m = mix[:, c, t * P:(t + 1) * P]
                    ins = v.tensor_tensor(m, m, bias1[:], ALU.add)
                steps.wait(ins)
                xt = panel(xs, G, 1, CT, c * CT).rearrange("p t d -> p (t d)")
                steps.wait(v.scalar_tensor_tensor(xt, mix[:, c], 0.0, xt, ALU.max, ALU.add))

            def normalise(G, layer, c):
                ve.wait_ge(token_rstd, G * NC + c + 1)
                for t in range(CT):
                    ins = v.tensor_scalar(xn[:, c * CT + t],
                                          panel(xs, G, layer, 1, c * CT + t).rearrange("p o d -> p (o d)"),
                                          mv[:, t, 0:1], rstd[:, t:t + 1], ALU.subtract, ALU.mult)
                ins.then_inc(xn_made, 1)

            def gates(G, layer, c):
                ve.wait_ge(gate_psum, G * NC + c + 1)
                bg = gate_b[:, layer * E:(layer + 1) * E].unsqueeze(1).broadcast_to([P, CT, E])
                steps.wait(v.tensor_tensor(lg[:], mix[:, c, 0:CT * E].rearrange("p (t e) -> p t e", e=E),
                                           bg, ALU.add))
                if layer == 0:
                    steps.wait(v.tensor_reduce(top[:], lg[:], AX.X, ALU.max))
                    v.tensor_tensor(lg[:], lg[:], top[:].unsqueeze(2).broadcast_to([P, CT, E]),
                                    ALU.subtract).then_inc(logits_made, 1)

            def softmax(G, c):
                ve.wait_ge(exp_made, G * NC + c + 1)
                steps.wait(v.tensor_reduce(top[:], pr[:], AX.X, ALU.add))
                steps.wait(v.reciprocal(inv[:], top[:]))
                steps.wait(v.tensor_tensor(pr[:], pr[:], inv[:].unsqueeze(2).broadcast_to([P, CT, E]),
                                           ALU.mult))

            def compare(score):
                other = score[:].unsqueeze(2).broadcast_to([P, CT, E, E])
                own = score[:].unsqueeze(3).broadcast_to([P, CT, E, E])
                steps.wait(v.tensor_tensor(cmp_gt[:], other, own, ALU.is_gt))
                v.tensor_tensor(cmp_eq[:], other, own, ALU.is_equal).then_inc(compared, 1)

            def choose(G, layer, c):
                ve.wait_ge(rank_made, G * NC + c + 1)
                steps.wait(v.tensor_reduce(rank[:], cmp_gt[:], AX.X, ALU.add))
                if layer == 0:
                    ins = v.scalar_tensor_tensor(cw[:], rank[:], TOPK - 0.5, pr[:], ALU.is_lt, ALU.mult)
                else:
                    ins = v.tensor_scalar(cw[:], rank[:], TOPK - 0.5, None, ALU.is_lt)
                steps.wait(ins)
                steps.wait(v.tensor_copy(cw_pair[:, :, 0:E], cw[:]))
                v.tensor_tensor(cw_pair[:, :, E:2 * E], cw[:], cw_pair[:, :, 0:E].bitcast(F32),
                                ALU.subtract).then_inc(cw_made, 1)

            def unit(G, c, e, tail):
                hidden = halves(e, tail)[0]
                u = G * UNITS + c * E + e
                for half in range(2):
                    if half == 0:
                        ve.wait_ge(cwb_psum, u + 1)
                    ve.wait_ge(gelu_made, 2 * u + half + 1)
                    v.tensor_tensor(hidden[:, half], hidden[:, half], cw_bank(e, tail),
                                    ALU.mult).then_inc(scaled, 1)

            def add(G, layer, c):
                ve.wait_ge(out_psum, G * NC + c + 1)
                xt = panel(xs, G, layer, CT, c * CT).rearrange("p t d -> p (t d)")
                v.tensor_tensor(xt, xt, mix[:, c], ALU.add).then_inc(out_added, 1)

            def run(G, kind, layer, e_layer, tiles=JB):
                for what, *n in schedule(kind, tiles, ahead(tiles)):
                    if what == "tile":
                        tile(G, n[0])
                        continue
                    back, c, *e = n
                    if what == "own_sum" and e_layer == 1:
                        own_sum(G - back, c)
                    elif what == "own_turn" and e_layer == 1:
                        turned(G - back, 1, 0, c)
                    elif what == "graph_out":
                        graph_out(G - back, e_layer, c)
                    elif what == "moments":
                        moments(G - back, e_layer, c * CT, CT, stats, mv, rstd, token_var)
                    elif what == "normalise":
                        normalise(G - back, e_layer, c)
                    elif what == "turn":
                        turned(G - back, e_layer, e_layer, c)
                    elif what == "gate":
                        gates(G - back, e_layer, c)
                    elif what == "softmax":
                        if e_layer == 0:
                            softmax(G - back, c)
                        compare(lg if e_layer else pr)
                    elif what == "choose":
                        choose(G - back, e_layer, c)
                    elif what == "unit":
                        unit(G - back, c, *e, not tiles)
                    elif what == "add":
                        add(G - back, e_layer, c)
                    elif kind == "first":
                        after(what, NP - 1, c)
                    elif what == "next1":
                        ve.wait_ge(out_added, back * NC + c + 1)
                        next1(NP + back, 1, c)
                    elif what == "next2":
                        next2((NP + back) * NC + c, NP + back, 1, c, False)

            def loop(first, layer):
                with ve.Fori(first, first + NP - 2) as G:
                    steps.loop(G, first, STEPS, NP - 2)
                    run(G, "steady", layer, layer)
                    steps.end_loop()

            run(0, "first", 0, 0)
            run(1, "second", 0, 0, JB - TT)
            for G in range(2, NP):
                run(G, "steady", 0, 0, JB - G * TT)
            run(NP, "finish", 1, 0)
            run(NP + 1, "second", 1, 1)
            loop(NP + 2, 1)
            run(2 * NP, "finish", 1, 1, tiles=0)


STEPS = 18


def program(nc, shapes):
    args = [nc.dram_tensor("in_" + name, shape, F32, kind="ExternalInput").ap() for name, shape in shapes]
    out = nc.dram_tensor("out", (P, JB, D), F32, kind="ExternalOutput").ap()
    two_layers(nc, *args, out)


def kernel(x, adj, L0_gnn_W, L0_ffn_gate_w, L0_ffn_gate_b, L0_ffn_W1, L0_ffn_b1, L0_ffn_W2, L0_ffn_b2,
           L1_gnn_weight, L1_gnn_bias, L1_ffn_Wg, L1_ffn_bg, L1_ffn_W1, L1_ffn_b1, L1_ffn_W2, L1_ffn_b2):
    import concourse.bacc as bacc
    from concourse.bass_utils import run_bass_kernel_spmd

    def lay(a):
        return np.ascontiguousarray(a)

    a = np.asarray(adj)
    weights = []
    for w1, w2 in ((L0_ffn_W1, L0_ffn_W2), (L1_ffn_W1, L1_ffn_W2)):
        w1 = np.asarray(w1).transpose(1, 0, 2).reshape(P, E * H)
        w2 = np.asarray(w2).reshape(E, 2, P, D).transpose(2, 0, 1, 3).reshape(P, E * H)
        weights.append(np.concatenate([w1, w2], 1).reshape(P, WT, PW).transpose(1, 0, 2))
    b1 = [np.asarray(b).reshape(E, 2, P).transpose(2, 0, 1).reshape(P, 2 * E) for b in (L0_ffn_b1, L1_ffn_b1)]
    b2 = [np.concatenate([np.asarray(b)] * 2) for b in (L0_ffn_b2, L1_ffn_b2)]
    gate_b = np.concatenate([np.asarray(L0_ffn_gate_b), np.asarray(L1_ffn_bg)])
    gnn1 = np.asarray(L1_gnn_weight)
    e = np.arange(E)
    arrays = {
        "x": lay(np.asarray(x).reshape(JB, P, D).transpose(1, 0, 2)),
        "adj_rows": lay(a.reshape(JB, P, 8, PW).transpose(0, 2, 1, 3)),
        "adj_cols": lay(a.reshape(NP, PW, JB, P).transpose(0, 2, 3, 1)),
        "w_gnn0": lay(np.asarray(L0_gnn_W).T),
        "w_gnn1_own": lay(gnn1[:D]),
        "w_gnn1_agg": lay(gnn1[D:]),
        "bias_gnn1": lay(np.broadcast_to(np.asarray(L1_gnn_bias), (P, D))),
        "w_experts": lay(np.stack(weights)),
        "b1": lay(np.stack(b1, 1)),
        "b2": lay(np.stack(b2, 1)),
        "w_gate": lay(np.concatenate([np.asarray(L0_ffn_gate_w), np.asarray(L1_ffn_Wg)], 1)),
        "b_gate": lay(np.broadcast_to(gate_b, (P, 2 * E))),
        "ident": np.eye(P, dtype=np.float32),
        "select": np.concatenate([np.eye(E, dtype=np.float32)] * 2),
        "below": lay(np.broadcast_to((e[None, :] < e[:, None]).astype(np.float32).reshape(-1), (P, E * E))),
    }
    nc = bacc.Bacc("TRN2", target_bir_lowering=False, num_devices=1, dynamic_dma_scratch_size=1024)
    program(nc, [(k, v.shape) for k, v in arrays.items()])
    r = run_bass_kernel_spmd(nc, [{"in_" + k: v for k, v in arrays.items()}], core_ids=[0])
    got = r.results[0]["out"]
    return got.transpose(1, 0, 2).reshape(N, D)
```
